# Optimizing a Trainium2 kernel written in Bass

```python
import numpy as np
import jax
import jax.numpy as jnp

def _softmax(x, axis=-1):
    return jax.nn.softmax(x, axis=axis)

def _gelu(x):
    return jax.nn.gelu(x, approximate=True)

def _silu(x):
    return jax.nn.silu(x)

def _sigmoid(x):
    return jax.nn.sigmoid(x)

def _layernorm(x, axis=-1, eps=1e-05):
    m = jnp.mean(x, axis=axis, keepdims=True)
    v = jnp.var(x, axis=axis, keepdims=True)
    return (x - m) / jnp.sqrt(v + eps)

def _scatter_add(tgt, idx, src, axis=0):
    return tgt.at[idx].add(src)

def _segment_sum(src, seg, n):
    return jax.ops.segment_sum(src, seg, n)
kernel_name = 'mk_early_fusion_d1_tok_img1024_r4_a06761'

def setup_inputs(seed: int=0):
    np.random.seed(seed)
    _w = jnp.asarray

    def _rec_inputs():
        import jax
        import jax.numpy as jnp
        _rk = jax.random.key(seed)
        x = -0.00016672 + 0.999947 * jax.random.normal(jax.random.fold_in(_rk, 1), (16, 3, 96, 96), jnp.float32)
        txt = 0.00140885 + 1.4139 * jax.random.normal(jax.random.fold_in(_rk, 2), (16, 77, 256), jnp.float32)
        return (x, txt)
    x, txt = _rec_inputs()

    def _L0_tok_setup():
        import jax, jax.numpy as jnp
        import numpy as np
        B, C, H, W = (64, 3, 96, 96)
        P = 16
        NP = H // P * (W // P)
        PD = C * P * P
        ED = 256
        NCLS = 1

        def _layernorm(x, g, b, eps=1e-05):
            mu = jnp.mean(x, axis=-1, keepdims=True)
            var = jnp.mean(jnp.square(x - mu), axis=-1, keepdims=True)
            return (x - mu) * jax.lax.rsqrt(var + eps) * g + b
        key = jax.random.key(seed)
        ks = jax.random.split(key, 8)
        x = jax.random.normal(ks[0], (B, C, H, W), dtype=jnp.float32)
        ln1_g = jnp.ones((PD,), jnp.float32)
        ln1_b = jnp.zeros((PD,), jnp.float32)
        W_proj = jax.random.normal(ks[1], (PD, ED), jnp.float32) / np.sqrt(PD)
        b_proj = jnp.zeros((ED,), jnp.float32)
        ln2_g = jnp.ones((ED,), jnp.float32)
        ln2_b = jnp.zeros((ED,), jnp.float32)
        cls_token = jax.random.normal(ks[2], (1, NCLS, ED), jnp.float32)
        pos_emb = jax.random.normal(ks[3], (1, NP + NCLS, ED), jnp.float32)
        return {'x': x, 'ln1_g': ln1_g, 'ln1_b': ln1_b, 'W_proj': W_proj, 'b_proj': b_proj, 'ln2_g': ln2_g, 'ln2_b': ln2_b, 'cls_token': cls_token, 'pos_emb': pos_emb}
    _L0_tok_all = _L0_tok_setup()
    _L0_tok_in = {k: v for k, v in _L0_tok_all.items() if k in ('ln1_g', 'ln1_b', 'W_proj', 'b_proj', 'ln2_g', 'ln2_b', 'cls_token', 'pos_emb')}
    del _L0_tok_all

    def _L0_attn_setup():
        import jax, jax.numpy as jnp
        import numpy as np
        N_EMBD = 256
        N_HEAD = 16
        DK = N_EMBD // N_HEAD
        key = jax.random.key(seed)
        k1, k2, k3 = jax.random.split(key, 3)
        x = jax.random.normal(k1, (2, 512, N_EMBD), dtype=jnp.float32)
        w_attn = jax.random.normal(k2, (3 * N_EMBD, N_EMBD), dtype=jnp.float32) * N_EMBD ** (-0.5)
        w_proj = jax.random.normal(k3, (N_EMBD, N_EMBD), dtype=jnp.float32) * N_EMBD ** (-0.5)
        return {'x': x, 'w_attn': w_attn, 'w_proj': w_proj}
    _L0_attn_all = _L0_attn_setup()
    _L0_attn_in = {k: v for k, v in _L0_attn_all.items() if k in ('w_attn', 'w_proj')}
    del _L0_attn_all

    def _L0_ffn_setup():
        import jax, jax.numpy as jnp
        import numpy as np
        NUM_EXPERTS = 8
        N_EMBD = 256
        D_FF = 4 * N_EMBD
        B, S = (4, 512)
        key = jax.random.key(seed)
        ks = jax.random.split(key, 6)
        x = jax.random.normal(ks[0], (B, S, N_EMBD), dtype=jnp.float32)
        gate_w = jax.random.normal(ks[1], (N_EMBD, NUM_EXPERTS), dtype=jnp.float32) * 0.02
        w1 = jax.random.normal(ks[2], (NUM_EXPERTS, N_EMBD, D_FF), dtype=jnp.float32) * 0.02
        b1 = jnp.zeros((NUM_EXPERTS, D_FF), dtype=jnp.float32)
        w2 = jax.random.normal(ks[3], (NUM_EXPERTS, D_FF, N_EMBD), dtype=jnp.float32) * 0.02
        b2 = jnp.zeros((NUM_EXPERTS, N_EMBD), dtype=jnp.float32)
        return {'x': x, 'gate_w': gate_w, 'w1': w1, 'b1': b1, 'w2': w2, 'b2': b2}
    _L0_ffn_all = _L0_ffn_setup()
    _L0_ffn_in = {k: v for k, v in _L0_ffn_all.items() if k in ('gate_w', 'w1', 'b1', 'w2', 'b2')}
    del _L0_ffn_all
    return {'x': x, 'txt': txt, 'L0_tok_ln1_g': _L0_tok_in['ln1_g'], 'L0_tok_ln1_b': _L0_tok_in['ln1_b'], 'L0_tok_W_proj': _L0_tok_in['W_proj'], 'L0_tok_b_proj': _L0_tok_in['b_proj'], 'L0_tok_ln2_g': _L0_tok_in['ln2_g'], 'L0_tok_ln2_b': _L0_tok_in['ln2_b'], 'L0_tok_cls_token': _L0_tok_in['cls_token'], 'L0_tok_pos_emb': _L0_tok_in['pos_emb'], 'L0_attn_w_attn': _L0_attn_in['w_attn'], 'L0_attn_w_proj': _L0_attn_in['w_proj'], 'L0_ffn_gate_w': _L0_ffn_in['gate_w'], 'L0_ffn_w1': _L0_ffn_in['w1'], 'L0_ffn_b1': _L0_ffn_in['b1'], 'L0_ffn_w2': _L0_ffn_in['w2'], 'L0_ffn_b2': _L0_ffn_in['b2']}

def reference(x, txt, L0_tok_ln1_g, L0_tok_ln1_b, L0_tok_W_proj, L0_tok_b_proj, L0_tok_ln2_g, L0_tok_ln2_b, L0_tok_cls_token, L0_tok_pos_emb, L0_attn_w_attn, L0_attn_w_proj, L0_ffn_gate_w, L0_ffn_w1, L0_ffn_b1, L0_ffn_w2, L0_ffn_b2):
    import jax
    import jax.numpy as jnp

    def _L0_tok_ref(x, ln1_g, ln1_b, W_proj, b_proj, ln2_g, ln2_b, cls_token, pos_emb):
        import jax, jax.numpy as jnp
        import numpy as np
        B, C, H, W = (64, 3, 96, 96)
        P = 16
        NP = H // P * (W // P)
        PD = C * P * P
        ED = 256
        NCLS = 1

        def _layernorm(x, g, b, eps=1e-05):
            mu = jnp.mean(x, axis=-1, keepdims=True)
            var = jnp.mean(jnp.square(x - mu), axis=-1, keepdims=True)
            return (x - mu) * jax.lax.rsqrt(var + eps) * g + b
        b = x.shape[0]
        h, w = (H // P, W // P)
        patches = x.reshape(b, C, h, P, w, P)
        patches = patches.transpose(0, 2, 4, 3, 5, 1).reshape(b, h * w, P * P * C)
        z = _layernorm(patches, ln1_g, ln1_b)
        z = jnp.einsum('bnp,pe->bne', z, W_proj) + b_proj
        z = _layernorm(z, ln2_g, ln2_b)
        cls = jnp.broadcast_to(cls_token, (b, NCLS, ED))
        z = jnp.concatenate([cls, z], axis=1)
        z = z + pos_emb
        return z

    def _L0_attn_ref(x, w_attn, w_proj):
        import jax, jax.numpy as jnp
        import numpy as np
        N_EMBD = 256
        N_HEAD = 16
        DK = N_EMBD // N_HEAD
        b, t, c = x.shape
        qkv = jnp.einsum('btc,oc->bto', x, w_attn)
        q, k, v = jnp.split(qkv, 3, axis=-1)
        q = q.reshape(b, t, N_HEAD, DK).transpose(0, 2, 1, 3)
        k = k.reshape(b, t, N_HEAD, DK).transpose(0, 2, 1, 3)
        v = v.reshape(b, t, N_HEAD, DK).transpose(0, 2, 1, 3)
        attn = jnp.einsum('bhqd,bhkd->bhqk', q, k) * DK ** (-0.5)
        mask = jnp.triu(jnp.ones((t, t), dtype=bool), k=1)
        attn = jnp.where(mask, -jnp.inf, attn)
        attn = jax.nn.softmax(attn, axis=-1)
        out = jnp.einsum('bhqk,bhkd->bhqd', attn, v)
        out = out.transpose(0, 2, 1, 3).reshape(b, t, c)
        out = jnp.einsum('btc,oc->bto', out, w_proj)
        return out

    def _L0_ffn_ref(x, gate_w, w1, b1, w2, b2):
        import jax, jax.numpy as jnp
        import numpy as np
        NUM_EXPERTS = 8
        N_EMBD = 256
        D_FF = 4 * N_EMBD
        B, S = (4, 512)
        Bb, Ss, D = x.shape
        x_flat = x.reshape(-1, D)
        router_logits = x_flat @ gate_w
        router_probs = jax.nn.softmax(router_logits, axis=-1)
        expert_idx = jnp.argmax(router_probs, axis=-1)
        expert_w = jnp.take_along_axis(router_probs, expert_idx[:, None], axis=1)[:, 0]
        out = jnp.zeros_like(x_flat)
        for e in range(NUM_EXPERTS):
            h = jax.nn.gelu(x_flat @ w1[e] + b1[e], approximate=False)
            y = h @ w2[e] + b2[e]
            sel = expert_idx == e
            out = out + jnp.where(sel, expert_w, 0.0)[:, None] * y
        return out.reshape(Bb, Ss, D)
    h = _L0_tok_ref(x, L0_tok_ln1_g, L0_tok_ln1_b, L0_tok_W_proj, L0_tok_b_proj, L0_tok_ln2_g, L0_tok_ln2_b, L0_tok_cls_token, L0_tok_pos_emb)
    h = jnp.concatenate([h, txt], axis=1)
    h = h + _L0_attn_ref(_layernorm(h, axis=-1), L0_attn_w_attn, L0_attn_w_proj)
    h = h + _L0_ffn_ref(_layernorm(h, axis=-1), L0_ffn_gate_w, L0_ffn_w1, L0_ffn_b1, L0_ffn_w2, L0_ffn_b2)
    return h

_drawn_inputs = setup_inputs


def setup_inputs(seed=0):
    import zlib

    import numpy as np

    out = dict(_drawn_inputs(seed))
    spreads = {'L0_tok_ln1_g': (1.0, 0.2),
     'L0_tok_ln1_b': (0.0, 0.1),
     'L0_tok_b_proj': (0.0, 0.1),
     'L0_tok_ln2_g': (1.0, 0.2),
     'L0_tok_ln2_b': (0.0, 0.1),
     'L0_ffn_b1': (0.0, 0.8),
     'L0_ffn_b2': (0.0, 0.598)}
    factors = {'L0_ffn_gate_w': 2.956, 'L0_ffn_w1': 3.903, 'L0_ffn_w2': 3.646}
    for name, (base, spread) in spreads.items():
        noise = np.random.default_rng([zlib.crc32(name.encode()), seed]).standard_normal(out[name].shape)
        drawn = base * np.exp(spread * noise) if base else spread * noise
        out[name] = jnp.asarray(drawn.astype(out[name].dtype))
    for name, factor in factors.items():
        out[name] = (out[name] * factor).astype(out[name].dtype)
    return out
```

```python
from contextlib import ExitStack

import concourse.bass as bass
from concourse import mybir

ALU = mybir.AluOpType
ACT = mybir.ActivationFunctionType
AX = mybir.AxisListType
F32 = mybir.dt.float32
BF16 = mybir.dt.bfloat16
I32 = mybir.dt.int32
U32 = mybir.dt.uint32
LN_EPS = 1e-5
MASKED = -1e30


def loop_by(unroll, eng, count, step):
    rest = count % unroll
    for n in range(unroll + rest):
        step(n, n % unroll)
    with eng.Fori(1, count // unroll) as i:
        for n in range(rest, rest + unroll):
            step(unroll * i + n, n % unroll)


def fusion_program(nc, x, txt, ln1_g, ln1_b, w_patch, b_patch, ln2_g, ln2_b, cls_token, pos_emb,
                   w_attn, w_proj, gate_w, w1, b1, w2, b2, out):
    B, C, HH, _ = x.shape
    S, E = txt.shape[1:]
    PS = 16
    G = HH // PS
    T = 1 + G * G + S
    R = B * G
    PD = C * PS * PS
    PC = PD // 128
    EC = E // 128
    H, DK = 16, E // 16
    X, _, F = w1.shape
    FC = F // 128
    SLOT = 128
    NBLK = (B * T + X * (SLOT - 1)) // SLOT
    NBLK += NBLK % 2
    NFULL = -(-B * T // SLOT)
    RES, WGT, TOK, ROW = E, 2 * E, 2 * E + 1, 2 * E + 4
    NOBODY = 1 << 20
    RING = 4
    HG = 4
    NG = H // HG

    sorted_rows = nc.dram_tensor("sorted_rows", [NBLK * SLOT, ROW], F32)
    patch_rows = nc.dram_tensor("patch_rows", [R, G, E], F32)
    out_rows = out.rearrange("b t d -> (b t) d")

    with ExitStack() as ctx:
        def sb(name, shape, dt=F32):
            return ctx.enter_context(nc.sbuf_tensor(name, shape, dt))

        def sem(name):
            return ctx.enter_context(nc.semaphore(name))

        experts = sb("experts", [128, X, EC * F + FC * E])
        w1_sb = experts[:, :, 0:EC * F].rearrange("p e (k f) -> p e k f", k=EC)
        w2_sb = experts[:, :, EC * F:].rearrange("p e (c d) -> p e c d", c=FC)
        rows = sb("rows", [T, B, ROW])

        def carver(room):
            taken = [0]

            def carve(width):
                taken[0] += width
                assert taken[0] <= room.shape[1]
                return room[:, taken[0] - width:taken[0]]
            return carve

        carve = carver(experts[:, X - 4:X - 1, :].rearrange("p e n -> p (e n)"))
        px = carve(C * PS * HH).rearrange("p (c n) -> p c n", c=C)[0:R]
        pxn = carve(2 * PD).rearrange("p (s n) -> p s n", s=2)[0:R]
        w_patch_sb = carve(PC * E).rearrange("p (c e) -> p c e", c=PC)
        w_nat = carve(4 * EC * E).rearrange("p (n e) -> p n e", n=4 * EC)
        b1_nat = carve(128)[0:X * FC]
        probs = experts[:, X - 1, 0:2 * H * T].rearrange("p (s h t) -> p s h t", s=2, h=H)[0:T]

        WORK = 7184
        work = sb("work", [128, WORK])
        carve = carver(work[:, :])
        pxT = carve(2 * PC * R).rearrange("p (s c r) -> p s c r", s=2, c=PC)
        pz = carve(2 * E).rearrange("p (s n) -> p s n", s=2)[0:R]
        b_patch_bc = carve(E)[0:R]
        ln2_g_bc = carve(E)[0:R]
        ln2_b_bc = carve(E)[0:R]
        pos_bc = carve(G * E).rearrange("p (w n) -> p w n", w=G)[0:R]
        cls_pos = carve(2 * E).rearrange("p (s n) -> p s n", s=2)[0:1]
        carve = carver(work[:, :])
        probsT = carve(H * T).rearrange("p (h t) -> p h t", h=H)[0:T]
        xn = carve(2 * E).rearrange("p (s n) -> p s n", s=2)[0:T]
        xnT = carve(2 * EC * T).rearrange("p (s k t) -> p s k t", s=2, k=EC)
        qT = carve(2 * EC * T).rearrange("p (s k t) -> p s k t", s=2, k=EC)
        kT_split = carve(2 * EC * 2 * T).rearrange("p (s k o t) -> p s k o t", s=2, k=EC, o=2)
        v_aug = carve(2 * H * (DK + 1)).rearrange("p (s h d) -> p s h d", s=2, h=H)[0:T]
        o_sb = carve(E)[0:T]
        oT = carve(EC * T).rearrange("p (k t) -> p k t", k=EC)
        x2 = carve(4 * E).rearrange("p (s n) -> p s n", s=2)[0:T]
        x2T = carve(EC * T).rearrange("p (k t) -> p k t", k=EC)
        carve = carver(work[:, :])
        hid = carve(2 * F).rearrange("p (s n) -> p s n", s=2)
        actT = carve(2 * F).rearrange("p (s c t) -> p s c t", s=2, c=FC)
        blk_out = carve(2 * E).rearrange("p (s n) -> p s n", s=2)
        blkT = carve(2 * E).rearrange("p (s c t) -> p s c t", s=2, c=EC)
        blk_in = carve(RING * ROW).rearrange("p (s n) -> p s n", s=RING)

        attn_w = sb("attn_w", [128, EC * 3 * E + EC * E])
        w_attnT = attn_w[:, 0:EC * 3 * E].rearrange("p (k n) -> p k n", k=EC)
        w_projT = attn_w[:, EC * 3 * E:].rearrange("p (k n) -> p k n", k=EC)
        b2_bc = attn_w[:, 0:X * E].rearrange("p (x e) -> p x e", x=X)

        gate_sb = sb("gate_sb", [128, EC, X])
        b1T = sb("b1T", [128, X * FC])
        ident = sb("ident", [128, 128])
        ident_bf = sb("ident_bf", [T, T], BF16)
        mask_bf = sb("mask_bf", [T, HG, T], BF16)
        before = sb("before", [T, T], BF16)
        ones_bf = sb("ones_bf", [T, T], BF16)
        part_no = sb("part_no", [128, 1], I32)
        part_bit = sb("part_bit", [128, 1], I32)
        parity_of = sb("parity_of", [128, 2])
        minus_half = sb("minus_half", [128, B])
        eps = sb("eps", [128, B])
        pg = sb("pg", [128, 2, C, PC // C])
        px_six = sb("px_six", [R, G, C, 6])
        pz_six = sb("pz_six", [R, G, 6])
        pmv = sb("pmv", [R, G, 2])
        prs = sb("prs", [R, G, 2])
        zmv = sb("zmv", [R, G, 2])
        zrs = sb("zrs", [R, G, 2])
        six1 = sb("six1", [T, B, 6])
        six2 = sb("six2", [T, 2, 6])
        mv1 = sb("mv1", [T, B, 2])
        rs1 = sb("rs1", [T, B, 2])
        mv2 = sb("mv2", [T, 2, 2])
        rs2 = sb("rs2", [T, 2, 2])
        smax = sb("smax", [T, 2, H])
        rsum = sb("rsum", [T, H])
        logits = sb("logits", [T, B, X])
        lmax = sb("lmax", [T, B])
        lexp = sb("lexp", [T, B, X])
        lsum = sb("lsum", [T, B])
        lkey = sb("lkey", [T, B, X])
        lfirst = sb("lfirst", [T, B])
        chosen = sb("chosen", [T, B, X])
        chosen_bf = sb("chosen_bf", [T, B, X], BF16)
        expert_no = sb("expert_no", [T, X])
        filled = sb("filled", [T, NFULL])
        many = sb("many", [T, X, NFULL])
        count = sb("count", [T, X])
        nblk = sb("nblk", [T, X])
        blk_end = sb("blk_end", [T, X])
        start = sb("start", [T, X])
        slot_of = sb("slot_of", [T, B, X])
        pos_f = sb("pos_f", [T, B])
        pos = sb("pos", [T, B], I32)
        blk_no = sb("blk_no", [1, NBLK])
        blk_cmp = sb("blk_cmp", [1, NBLK, X])
        blk_ex_f = sb("blk_ex_f", [1, NBLK])
        blk_ex = sb("blk_ex", [1, NBLK], I32)
        empty_row = sb("empty_row", [128, ROW])
        ones_f = sb("ones_f", [T, X])

        bank = [ctx.enter_context(nc.psum_tensor(f"bank{i}", [128, 512], F32)) for i in range(8)]

        ld_x = [sem(f"ld_x{c}") for c in range(C)]
        ld_patch = sem("ld_patch")
        ld_const = sem("ld_const")
        ld_nat = sem("ld_nat")
        ld_cls = sem("ld_cls")
        ld_txt = sem("ld_txt")
        ld_tok = sem("ld_tok")
        ld_w = [sem(f"ld_w{e}") for e in range(X)]
        st_patch = [sem("st_patch0"), sem("st_patch1")]
        st_empty = sem("st_empty")
        st_rows = sem("st_rows")
        ld_blk = [sem(f"ld_blk{s}") for s in range(RING)]
        ld_b2 = sem("ld_b2")
        st_out = [sem("st_out0"), sem("st_out1")]
        pool_const = sem("pool_const")
        pool_chain = sem("pool_chain")
        dve_const = sem("dve_const")
        dve_chain = sem("dve_chain")
        cls_done = sem("cls_done")
        v_ones = sem("v_ones")
        px_stats = sem("px_stats")
        px_rstd = sem("px_rstd")
        px_norm = sem("px_norm")
        px_T = sem("px_T")
        px_Tcopied = sem("px_Tcopied")
        pz_ps = sem("pz_ps")
        pz_biased = sem("pz_biased")
        pz_stats = sem("pz_stats")
        pz_rstd = sem("pz_rstd")
        pz_normed = sem("pz_normed")
        pz_scaled = sem("pz_scaled")
        pz_done = sem("pz_done")
        px_pool = sem("px_pool")
        pz_pool = sem("pz_pool")
        p_chain = sem("p_chain")
        pz_chain = sem("pz_chain")
        posb_done = sem("posb_done")
        wT_ps = sem("wT_ps")
        wT_copied = sem("wT_copied")
        ln1_chain = sem("ln1_chain")
        ln1_stats = sem("ln1_stats")
        ln1_pool = sem("ln1_pool")
        xn_scaled = sem("xn_scaled")
        xn_ready = sem("xn_ready")
        xnT_ps = sem("xnT_ps")
        xnT_copied = sem("xnT_copied")
        qk_ps = sem("qk_ps")
        qk_copied = sem("qk_copied")
        v_ps = sem("v_ps")
        v_copied = sem("v_copied")
        scores_ps = sem("scores_ps")
        max_done = sem("max_done")
        shifted = sem("shifted")
        exp_done = sem("exp_done")
        pT_ps = sem("pT_ps")
        pT_copied = sem("pT_copied")
        pv_ps = sem("pv_ps")
        rsum_done = sem("rsum_done")
        o_done = sem("o_done")
        oT_ps = sem("oT_ps")
        oT_copied = sem("oT_copied")
        proj_ps = sem("proj_ps")
        resid_done = sem("resid_done")
        ln2_chain = sem("ln2_chain")
        ln2_stats = sem("ln2_stats")
        ln2_pool = sem("ln2_pool")
        x2n_ready = sem("x2n_ready")
        x2_kept = sem("x2_kept")
        x2T_ps = sem("x2T_ps")
        x2T_copied = sem("x2T_copied")
        logit_ps = sem("logit_ps")
        logit_kept = sem("logit_kept")
        r_chain = sem("r_chain")
        l_shifted = sem("l_shifted")
        l_exp = sem("l_exp")
        chosen_done = sem("chosen_done")
        rank_ps = sem("rank_ps")
        pos_done = sem("pos_done")
        weight_done = sem("weight_done")
        blk_ex_done = sem("blk_ex_done")
        blkT_ps = sem("blkT_ps")
        blkT_copied = sem("blkT_copied")
        hid_ps = sem("hid_ps")
        hid_copied = sem("hid_copied")
        hidT_ps = sem("hidT_ps")
        gelu_done = sem("gelu_done")
        y_ps = sem("y_ps")
        y_biased = sem("y_biased")
        blk_done = sem("blk_done")

        LN1_GROUPS = (range(0, 2), range(2, B))

        def head_at(n):
            g, j = n // HG, n % HG
            return H // EC * (j // 2) + 2 * g + j % 2

        PATCH_LOADS = 16 * (PC // C + 2 * (PC // C) + 3 + 1)

        def attention_steps(eng, step):
            def at(s, par):
                if isinstance(s, int):
                    step(s if s < B else None, s - 2 if 0 <= s - 2 < B else None,
                         s - 3 if 0 <= s - 3 < B else None, par)
                else:
                    step(s, s - 2, s - 3, par)
            for s in range(4):
                at(s, s % 2)
            with eng.Fori(2, B // 2 - 1) as i:
                at(2 * i, 0)
                at(2 * i + 1, 1)
            for s in range(B - 2, B + 3):
                at(s, s % 2)

        def early(index, least):
            return isinstance(index, int) and index < least

        block = ctx.enter_context(nc.Block())

        @block.sync
        def _(sp):
            xv = x.rearrange("b c (h p) w -> c b h (p w)", p=PS)
            for c in range(C):
                sp.dma_start(px[:, c, :], xv[c]).then_inc(ld_x[c], 16)
            sp.dma_start(rows[T - S:T, :, RES:RES + E], txt.rearrange("b s e -> s b e")).then_inc(ld_txt, 16)
            sp.wait_ge(cls_done, 1)
            sp.dma_start(rows[0:1, :, RES:RES + E], cls_pos[:, 0:1, :].to_broadcast([1, B, E])).then_inc(ld_txt, 16)
            for w in range(G):
                sp.wait_ge(pz_done, w + 1)
                sp.dma_start(patch_rows[:, w, :], pz[:, w % 2, :]).then_inc(st_patch[w % 2], 16)
            for par in range(2):
                sp.wait_ge(st_patch[par], 8 * G)
            sp.dma_start(rows[1:1 + G * G, :, RES:RES + E],
                         patch_rows.rearrange("(b h) w e -> (h w) b e", b=B)).then_inc(ld_tok, 16)
            sp.wait_ge(wT_copied, 4 * EC + 1)
            for e in range(X - 1):
                sp.dma_start(w1_sb[:, e], w1[e].rearrange("(k p) f -> p k f", p=128)).then_inc(ld_w[e], 16)
                sp.dma_start(w2_sb[:, e], w2[e].rearrange("(c p) d -> p c d", p=128)).then_inc(ld_w[e], 16)
            sp.wait_ge(pT_ps, NG * B)
            sp.dma_start(w1_sb[:, X - 1], w1[X - 1].rearrange("(k p) f -> p k f", p=128)).then_inc(ld_w[X - 1], 16)
            sp.dma_start(w2_sb[:, X - 1], w2[X - 1].rearrange("(c p) d -> p c d", p=128)).then_inc(ld_w[X - 1], 16)
            sp.wait_ge(proj_ps, B)
            sp.dma_start(b2_bc, b2.partition_broadcast(128)).then_inc(ld_b2, 16)

            def load_block(k, slot):
                if not early(k, RING):
                    sp.wait_ge(st_out[slot % 2], 8 * (k - RING - slot % 2) + 16)
                sp.dma_start(blk_in[:, slot, :], sorted_rows[bass.ds(k * SLOT, SLOT), :]).then_inc(ld_blk[slot], 16)

            sp.wait_ge(st_rows, 16 * B)
            loop_by(RING, sp, NBLK, load_block)

        @block.gpsimd
        def _(pool):
            pool.memset(ident[:, :], 0.0).then_inc(pool_chain, 1)
            pool.memset(ident_bf[:, :], 0.0).then_inc(pool_chain, 1)
            pool.memset(mask_bf[:, :, :], 0.0).then_inc(pool_chain, 1)
            pool.memset(before[:, :], 1.0).then_inc(pool_chain, 1)
            pool.memset(ones_bf[:, :], 1.0).then_inc(pool_const, 1)
            pool.memset(ones_f[:, :], 1.0).then_inc(pool_const, 1)
            pool.memset(minus_half[:, :], -0.5)
            pool.memset(eps[:, :], LN_EPS).then_inc(pool_const, 1)
            pool.memset(empty_row[:, :], 0.0).then_inc(pool_chain, 1)
            pool.wait_ge(pool_chain, 5)
            pool.affine_select(out=ident[:, :], in_=ident[:, :], compare_op=ALU.not_equal, fill=1.0,
                               base=0, pattern=[[-1, 128]], channel_multiplier=1).then_inc(pool_const, 1)
            pool.affine_select(out=ident_bf[:, :], in_=ident_bf[:, :], compare_op=ALU.not_equal, fill=1.0,
                               base=0, pattern=[[-1, T]], channel_multiplier=1).then_inc(pool_const, 1)
            pool.affine_select(out=mask_bf[:, :, :], in_=mask_bf[:, :, :], compare_op=ALU.is_ge, fill=MASKED,
                               base=0, pattern=[[0, HG], [-1, T]], channel_multiplier=1).then_inc(pool_const, 1)
            pool.affine_select(out=before[:, :], in_=before[:, :], compare_op=ALU.is_gt, fill=0.0,
                               base=0, pattern=[[1, T]], channel_multiplier=-1).then_inc(pool_const, 1)
            pool.iota(part_no[:, :], pattern=[[0, 1]], base=0, channel_multiplier=1).then_inc(pool_const, 1)
            pool.iota(expert_no[:, :], pattern=[[1, X]], base=0, channel_multiplier=0,
                      allow_small_or_imprecise_dtypes=True).then_inc(pool_const, 1)
            pool.iota(filled[:, :], pattern=[[SLOT, NFULL]], base=0, channel_multiplier=0,
                      allow_small_or_imprecise_dtypes=True).then_inc(pool_const, 1)
            pool.iota(blk_no[:, :], pattern=[[1, NBLK]], base=0, channel_multiplier=0,
                      allow_small_or_imprecise_dtypes=True).then_inc(pool_const, 1)
            pool.iota(rows[:, :, TOK].bitcast(I32), pattern=[[T, B]], base=0, channel_multiplier=1)\
                .then_inc(pool_const, 1)
            pool.iota(empty_row[:, TOK:TOK + 1].bitcast(I32), pattern=[[0, 1]], base=NOBODY,
                      channel_multiplier=0).then_inc(pool_const, 1)
            pool.memset(rows[:, :, TOK + 1:ROW], 0.0).then_inc(pool_const, 1)
            pool.wait_ge(pool_const, 14)
            for k in range(NBLK):
                pool.dma_start(sorted_rows[k * SLOT:(k + 1) * SLOT, :], empty_row[:, :]).then_inc(st_empty, 16)

            def rstd(mv, rs, chain, base):
                n, m, _ = mv.shape
                pool.tensor_tensor(rs[:, :, 1], mv[:, :, 1], eps[0:n, 0:m], ALU.add).then_inc(chain, 1)
                pool.wait_ge(chain, base + 1)
                pool.tensor_tensor(rs[:, :, 0], rs[:, :, 1], minus_half[0:n, 0:m], ALU.pow).then_inc(chain, 1)
                pool.wait_ge(chain, base + 2)
                return pool.tensor_tensor(rs[:, :, 1], mv[:, :, 0], rs[:, :, 0], ALU.mult)

            pool.wait_ge(ld_patch, PATCH_LOADS)
            for w in range(G):
                ins = pool.tensor_tensor(pos_bc[:, w, :], pos_bc[:, w, :], ln2_b_bc, ALU.add)
            ins.then_inc(posb_done, 1)
            for w in range(G + 2):
                if w < G:
                    pool.wait_ge(px_stats, w + 1)
                    rstd(pmv[:, w:w + 1, :], prs[:, w:w + 1, :], px_pool, 2 * w).then_inc(px_rstd, 1)
                if w >= 2:
                    pool.wait_ge(pz_stats, w - 1)
                    rstd(zmv[:, w - 2:w - 1, :], zrs[:, w - 2:w - 1, :], pz_pool, 2 * (w - 2)).then_inc(pz_rstd, 1)
            for par in range(2):
                pool.wait_ge(st_patch[par], 8 * G)
            pool.wait_ge(ld_txt, 32)
            pool.memset(v_aug[:, :, :, :], 1.0).then_inc(v_ones, 1)

            def ln1_rstd(n):
                g = slice(LN1_GROUPS[n].start, LN1_GROUPS[n].stop)
                pool.wait_ge(ln1_stats, n + 1)
                rstd(mv1[:, g, :], rs1[:, g, :], ln1_pool, 3 * n).then_inc(ln1_pool, 1)
                pool.wait_ge(ln1_pool, 3 * n + 3)

            def normalise(n, par):
                pool.tensor_tensor(xn[:, par, :], rows[:, n, RES:RES + E],
                                   rs1[:, n, 0:1].to_broadcast([T, E]), ALU.mult).then_inc(xn_scaled, 1)
                pool.wait_ge(xn_scaled, n + 1)
                pool.tensor_tensor(xn[:, par, :], xn[:, par, :],
                                   rs1[:, n, 1:2].to_broadcast([T, E]), ALU.subtract).then_inc(xn_ready, 1)

            ln1_rstd(0)
            normalise(0, 0)
            normalise(1, 1)
            ln1_rstd(1)

            def attention(f, b, r, par):
                if f is not None and not early(f, 1) and not (isinstance(f, int) and f + 1 >= B):
                    pool.wait_ge(xnT_ps, f)
                    normalise(f + 1, 1 - par)
                if b is not None:
                    pool.wait_ge(ln2_stats, b + 1)
                    rstd(mv2[:, par:par + 1, :], rs2[:, par:par + 1, :], ln2_pool, 4 * b).then_inc(ln2_pool, 1)
                    pool.wait_ge(ln2_pool, 4 * b + 3)
                    if not early(b, 2):
                        pool.wait_ge(x2T_ps, b - 1)
                    pool.tensor_tensor(x2[:, par, 0:E], x2[:, par, RES:RES + E],
                                       rs2[:, par, 0:1].to_broadcast([T, E]), ALU.mult).then_inc(ln2_pool, 1)
                    pool.wait_ge(ln2_pool, 4 * b + 4)
                    pool.tensor_tensor(x2[:, par, 0:E], x2[:, par, 0:E],
                                       rs2[:, par, 1:2].to_broadcast([T, E]), ALU.subtract).then_inc(x2n_ready, 1)
                    pool.wait_ge(x2n_ready, b + 1)
                    pool.tensor_copy(rows[:, b, 0:2 * E], x2[:, par, :]).then_inc(x2_kept, 1)

            attention_steps(pool, attention)

            pool.wait_ge(st_empty, 16 * NBLK)
            pool.wait_ge(x2_kept, B)
            pool.wait_ge(resid_done, B)
            pool.wait_ge(weight_done, 1)
            pool.wait_ge(pos_done, 1)
            for b in range(B):
                pool.indirect_dma_start(
                    out=sorted_rows[:, :], out_offset=bass.IndirectOffsetOnAxis(ap=pos[:, b:b + 1].bitcast(U32), axis=0),
                    in_=rows[:, b, :], in_offset=None).then_inc(st_rows, 16)

            last_row = pool.to_reg(B * T - 1)

            def store_block(k, par):
                pool.wait_ge(blk_done, k + 1)
                pool.indirect_dma_start(
                    out=out_rows, out_offset=bass.IndirectOffsetOnAxis(
                        ap=blk_in[:, k % RING, TOK:TOK + 1].bitcast(U32), axis=0),
                    in_=blk_out[:, par, :], in_offset=None,
                    bounds_check=last_row, oob_is_err=False).then_inc(st_out[par], 16)

            for k in range(NBLK):
                store_block(k, k % 2)
            for par in range(2):
                pool.wait_ge(st_out[par], 16 * (NBLK // 2))

        @block.scalar
        def _(act):
            for u in range(PC // C):
                act.dma_start(w_patch_sb.rearrange("k (c u) e -> k u c e", c=C)[:, u],
                              w_patch.rearrange("(u k c) e -> u k c e", u=PC // C, c=C)[u]).then_inc(ld_patch, 16)
            with nc.allow_non_contiguous_dma(reason="two short vectors, once"):
                for n, vec in enumerate((ln1_g, ln1_b)):
                    for u in range(PC // C):
                        act.dma_start(pg[:, n, :, u],
                                      vec.rearrange("(u k c) -> u k c", u=PC // C, c=C)[u])\
                            .then_inc(ld_patch, 16)
            for dst, vec in ((b_patch_bc, b_patch), (ln2_g_bc, ln2_g), (ln2_b_bc, ln2_b)):
                act.dma_start(dst, vec.partition_broadcast(R))\
                   .then_inc(ld_patch, 16)
            pos_v = pos_emb[0, 1:1 + G * G, :].rearrange("(a h w) e -> a h (w e)", a=1, w=G)
            act.dma_start(pos_bc.rearrange("r w e -> r (w e)"), pos_v.to_broadcast([B, G, G * E]))\
               .then_inc(ld_patch, 16)
            act.dma_start(w_nat[:, 0:3 * EC, :], w_attn.rearrange("(m p) e -> p m e", p=128)).then_inc(ld_nat, 16)
            act.dma_start(w_nat[:, 3 * EC:, :], w_proj.rearrange("(m p) e -> p m e", p=128)).then_inc(ld_nat, 16)
            act.dma_start(cls_pos[:, 0, :], cls_token[0]).then_inc(ld_cls, 16)
            act.dma_start(cls_pos[:, 1, :], pos_emb[0, 0:1, :]).then_inc(ld_cls, 16)
            act.dma_start(gate_sb[:, :, :], gate_w.rearrange("(k p) x -> p k x", p=128)).then_inc(ld_const, 16)
            act.dma_start(b1_nat[:, :], b1.rearrange("x (c p) -> (x c) p", p=128)).then_inc(ld_const, 16)

            act.wait_ge(ld_patch, PATCH_LOADS)

            def patch_evict(w, par):
                act.wait_ge(px_T, w + 1)
                if not early(w, 2):
                    act.wait_ge(pz_ps, w - 1)
                for c in range(PC):
                    src = bank[2 * par + c // 3][:, (c % 3) * R:(c % 3 + 1) * R]
                    ins = act.activation(pxT[:, par, c, :], src, ACT.Identity,
                                         bias=pg[:, 1, c // 2, c % 2:c % 2 + 1],
                                         scale=pg[:, 0, c // 2, c % 2:c % 2 + 1])
                ins.then_inc(px_Tcopied, 1)

            loop_by(2, act, G, patch_evict)

            for n in range(3 * EC + EC):
                act.wait_ge(wT_ps, n + 1)
                dst = w_attnT[:, :, n * 128:(n + 1) * 128] if n < 3 * EC else \
                    w_projT[:, :, (n - 3 * EC) * 128:(n - 3 * EC + 1) * 128]
                act.activation(dst, bank[6][:, 0:EC * 128].rearrange("p (k n) -> p k n", k=EC),
                               ACT.Copy).then_inc(wT_copied, 1)
            act.wait_ge(wT_ps, 4 * EC + 1)
            act.activation(b1T[:, :], bank[6][:, 0:X * FC], ACT.Copy).then_inc(wT_copied, 1)
            act.wait_ge(dve_const, 1)
            act.wait_ge(v_ones, 1)

            def attention(f, b, r, par):
                A, BB = bank[0], bank[1]
                if f is not None:
                    act.wait_ge(xnT_ps, f + 1)
                    if not early(f, 2):
                        act.wait_ge(v_ps, f - 1)
                    act.activation(xnT[:, par, :, :], A[:, 0:EC * T].rearrange("p (k t) -> p k t", k=EC),
                                   ACT.Copy).then_inc(xnT_copied, 1)

                def copy_pT(g):
                    act.wait_ge(pT_ps, NG * b + g + 1)
                    if g == 0 and not early(b, 1):
                        act.wait_ge(pv_ps, b)
                    act.activation(probsT[:, HG * g:HG * (g + 1), :],
                                   bank[6 + g % 2][0:T, 0:HG * T].rearrange("p (h t) -> p h t", h=HG),
                                   ACT.Copy).then_inc(pT_copied, 1)

                if b is not None:
                    copy_pT(0)
                    copy_pT(1)
                if f is not None:
                    act.wait_ge(qk_ps, f + 1)
                    if not early(f, 2):
                        act.wait_ge(scores_ps, NG * (f - 1))
                    qk = A[:, 0:2 * EC * T].rearrange("p (n k t) -> p n k t", n=2, k=EC)
                    act.activation(qT[:, par, :, :], qk[:, 0], ACT.Copy)
                    act.activation(kT_split[:, par, :, 0, :], qk[:, 1], ACT.Copy, scale=parity_of[:, 0:1])
                    act.activation(kT_split[:, par, :, 1, :], qk[:, 1], ACT.Copy, scale=parity_of[:, 1:2])\
                       .then_inc(qk_copied, 1)
                if b is not None:
                    copy_pT(2)
                    copy_pT(3)
                if f is not None:
                    act.wait_ge(v_ps, f + 1)
                    if not early(f, 2):
                        act.wait_ge(pv_ps, f - 1)
                    act.activation(v_aug[:, par, :, 0:DK],
                                   BB[0:T, 0:E].rearrange("p (h d) -> p h d", h=H), ACT.Copy)\
                       .then_inc(v_copied, 1)
                if b is not None:
                    act.wait_ge(oT_ps, b + 1)
                    if not early(b, 1):
                        act.wait_ge(proj_ps, b)
                    act.activation(oT[:, :, :], BB[:, 0:EC * T].rearrange("p (k t) -> p k t", k=EC),
                                   ACT.Copy).then_inc(oT_copied, 1)
                if r is not None:
                    act.wait_ge(x2T_ps, r + 1)
                    if not early(r, 1):
                        act.wait_ge(logit_ps, r)
                    act.activation(x2T[:, :, :], A[:, 0:EC * T].rearrange("p (k t) -> p k t", k=EC),
                                   ACT.Copy).then_inc(x2T_copied, 1)
                if f is not None:
                    for g in range(NG):
                        act.wait_ge(shifted, NG * f + g + 1)
                        p = probs[:, par, HG * g:HG * (g + 1), :]
                        act.activation(p, p, ACT.Exp, scale=float(DK) ** -0.5).then_inc(exp_done, 1)

            attention_steps(act, attention)

            act.wait_ge(l_shifted, 1)
            act.activation(lexp[:, :, :], lexp[:, :, :], ACT.Exp).then_inc(l_exp, 1)

            act.wait_ge(blk_ex_done, 1)

            def expert(k, par):
                e = act.value_load(blk_ex[0:1, bass.ds(k, 1)], min_val=0, max_val=X - 1)
                for c in range(FC):
                    if c % 4 == 0:
                        act.wait_ge(hidT_ps, 2 * k + c // 4 + 1)
                        if not early(k, 2):
                            act.wait_ge(y_ps, k - 1)
                    ins = act.activation(actT[:, par, c, :], bank[4 + c // 4][:, c % 4 * 128:(c % 4 + 1) * 128],
                                         ACT.Gelu, bias=b1T[:, bass.ds(e * FC + c, 1)])
                    if c % 4 == 3:
                        ins.then_inc(gelu_done, 1)

            loop_by(2, act, NBLK, expert)

        @block.tensor
        def _(pe):
            pe.wait_ge(pool_const, 7)

            def patch_T(w, par):
                pe.wait_ge(px_norm, w + 1)
                if not early(w, 2):
                    pe.wait_ge(px_Tcopied, w - 1)
                for c in range(PC):
                    ins = pe.transpose(bank[2 * par + c // 3][:, (c % 3) * R:(c % 3 + 1) * R],
                                       pxn[:, par, c * 128:(c + 1) * 128], ident[0:R, 0:R])
                ins.then_inc(px_T, 1)

            def patch_mm(w, par):
                pe.wait_ge(px_Tcopied, w + 1)
                if not early(w, 2):
                    pe.wait_ge(pz_biased, w - 1)
                for c in range(PC):
                    ins = pe.matmul(bank[4 + par][0:R, 0:E], pxT[:, par, c, :], w_patch_sb[:, c, :],
                                    start=(c == 0), stop=(c == PC - 1))
                ins.then_inc(pz_ps, 1)

            patch_T(0, 0)
            pe.wait_ge(ld_patch, PATCH_LOADS)
            patch_T(1, 1)
            patch_mm(0, 0)
            with pe.Fori(1, G // 2) as i:
                patch_T(2 * i, 0)
                patch_mm(2 * i - 1, 1)
                patch_T(2 * i + 1, 1)
                patch_mm(2 * i, 0)
            patch_mm(G - 1, 1)

            for n in range(4 * EC):
                if n == 0:
                    pe.wait_ge(ld_nat, 32)
                if n >= 1:
                    pe.wait_ge(wT_copied, n)
                for k in range(EC):
                    ins = pe.transpose(bank[6][:, k * 128:(k + 1) * 128],
                                       w_nat[:, n, k * 128:(k + 1) * 128], ident[:, :])
                ins.then_inc(wT_ps, 1)
            pe.wait_ge(wT_copied, 4 * EC)
            pe.wait_ge(ld_const, 32)
            pe.transpose(bank[6][:, 0:X * FC], b1_nat[:, :], ident[0:X * FC, 0:X * FC]).then_inc(wT_ps, 1)
            pe.wait_ge(wT_copied, 4 * EC + 1)

            def attention(f, b, r, par):
                A, BB = bank[0], bank[1]

                def probs_T(g):
                    pe.wait_ge(exp_done, NG * b + g + 1)
                    if not (early(b, 1) and g < 2):
                        pe.wait_ge(pT_copied, NG * b + g - 1)
                    for j in range(HG):
                        ins = pe.transpose(bank[6 + g % 2][0:T, j * T:(j + 1) * T],
                                           probs[:, par, HG * g + j, :], ident[0:T, 0:T])
                    ins.then_inc(pT_ps, 1)

                if f is not None:
                    pe.wait_ge(xn_ready, f + 1)
                    if early(f, 1):
                        pe.wait_ge(px_Tcopied, G)
                        pe.wait_ge(pz_biased, G)
                    if not early(f, 4):
                        pe.wait_ge(logit_kept, f - 3)
                    for k in range(EC):
                        ins = pe.transpose(A[:, k * T:(k + 1) * T], xn[:, par, k * 128:(k + 1) * 128],
                                           ident[0:T, 0:T])
                    ins.then_inc(xnT_ps, 1)
                if b is not None:
                    probs_T(0)
                    probs_T(1)
                if f is not None:
                    pe.wait_ge(xnT_copied, f + 1)
                    for m in range(2 * EC):
                        for k in range(EC):
                            ins = pe.matmul(A[:, m * T:(m + 1) * T], w_attnT[:, k, m * 128:(m + 1) * 128],
                                            xnT[:, par, k, :], start=(k == 0), stop=(k == EC - 1))
                    ins.then_inc(qk_ps, 1)
                if b is not None:
                    probs_T(2)
                    probs_T(3)
                    pe.wait_ge(pT_copied, NG * (b + 1))
                    pe.wait_ge(v_copied, b + 1)
                    if f is not None:
                        pe.wait_ge(qk_copied, f + 1)
                    else:
                        pe.wait_ge(logit_kept, b - 1)
                    for n in range(H):
                        h = head_at(n)
                        ins = pe.matmul(A[0:T, h * (DK + 1):(h + 1) * (DK + 1)], probsT[:, n, :],
                                        v_aug[:, par, h, :], start=True, stop=True)
                    ins.then_inc(pv_ps, 1)
                if f is not None:
                    if not early(f, 3):
                        pe.wait_ge(resid_done, f - 2)
                    for k in range(EC):
                        ins = pe.matmul(BB[0:T, 0:E], xnT[:, par, k, :], w_attnT[:, k, 2 * E:3 * E],
                                        start=(k == 0), stop=(k == EC - 1))
                    ins.then_inc(v_ps, 1)
                    pe.wait_ge(qk_copied, f + 1)
                    for g in range(NG):
                        if not early(f, 1):
                            pe.wait_ge(shifted, NG * (f - 1) + g + 1)
                        pe.matmul(bank[2 + g][0:T, 0:HG * T], ident_bf[:, :],
                                  mask_bf[:, :, :].rearrange("p h t -> p (h t)"), start=True, stop=False)
                    for c in range(EC):
                        for g in range(NG):
                            ins = pe.matmul(bank[2 + g][0:T, 2 * c * T:2 * (c + 1) * T],
                                            qT[32 * g:32 * g + 32, par, c, :],
                                            kT_split[32 * g:32 * g + 32, par, c, :, :].rearrange("p o t -> p (o t)"),
                                            start=False, stop=(c == EC - 1))
                            if c == EC - 1:
                                ins.then_inc(scores_ps, 1)
                if b is not None:
                    pe.wait_ge(o_done, b + 1)
                    if f is not None:
                        pe.wait_ge(v_copied, f + 1)
                    else:
                        pe.wait_ge(resid_done, b)
                    for k in range(EC):
                        ins = pe.transpose(BB[:, k * T:(k + 1) * T], o_sb[:, k * 128:(k + 1) * 128],
                                           ident[0:T, 0:T])
                    ins.then_inc(oT_ps, 1)
                if r is not None:
                    pe.wait_ge(x2n_ready, r + 1)
                    if b is None:
                        pe.wait_ge(logit_kept, r)
                    for k in range(EC):
                        ins = pe.transpose(A[:, k * T:(k + 1) * T], x2[:, 1 - par, k * 128:(k + 1) * 128],
                                           ident[0:T, 0:T])
                    ins.then_inc(x2T_ps, 1)
                if b is not None:
                    pe.wait_ge(oT_copied, b + 1)
                    for k in range(EC):
                        ins = pe.matmul(BB[0:T, 0:E], oT[:, k, :], w_projT[:, k, :],
                                        start=(k == 0), stop=(k == EC - 1))
                    ins.then_inc(proj_ps, 1)
                if r is not None:
                    pe.wait_ge(x2T_copied, r + 1)
                    for k in range(EC):
                        ins = pe.matmul(A[0:T, 0:X], x2T[:, k, :], gate_sb[:, k, :],
                                        start=(k == 0), stop=(k == EC - 1))
                    ins.then_inc(logit_ps, 1)

            attention_steps(pe, attention)

            pe.wait_ge(chosen_done, 1)
            picks = chosen_bf[:, :, :].rearrange("p b x -> p (b x)")
            pe.matmul(bank[0][0:T, 0:B * X], before[:, :], picks, start=True, stop=False)
            for d in range(1, B):
                ins = pe.matmul(bank[0][0:T, d * X:B * X], ones_bf[:, :], picks[:, 0:(B - d) * X],
                                start=False, stop=(d == B - 1))
            pe.matmul(bank[1][0:T, 0:B * X], ones_bf[:, :], picks, start=True, stop=True).then_inc(rank_ps, 1)

            pe.wait_ge(blk_ex_done, 1)
            for e in range(X):
                pe.wait_ge(ld_w[e], 32)

            def block_T(k, slot):
                pe.wait_ge(ld_blk[slot], 16 // RING * (k - slot) + 16)
                if not early(k, 1):
                    pe.wait_ge(blkT_copied, k)
                for c in range(EC):
                    ins = pe.transpose(bank[6][:, c * 128:(c + 1) * 128],
                                       blk_in[:, slot, c * 128:(c + 1) * 128], ident[:, :])
                ins.then_inc(blkT_ps, 1)

            def hidden(k, par):
                e = pe.value_load(blk_ex[0:1, bass.ds(k, 1)], min_val=0, max_val=X - 1)
                pe.wait_ge(blkT_copied, k + 1)
                if not early(k, 2):
                    pe.wait_ge(hid_copied, 2 * (k - 1))
                for n in range(F // 512):
                    for c in range(EC):
                        ins = pe.matmul(bank[2 * par + n][:, :], blkT[:, par, c, :],
                                        w1_sb[:, bass.ds(e, 1), c, n * 512:(n + 1) * 512],
                                        start=(c == 0), stop=(c == EC - 1))
                    ins.then_inc(hid_ps, 1)

            def hidden_T(k, par):
                for n in range(2):
                    pe.wait_ge(hid_copied, 2 * k + n + 1)
                    if not early(k, 1):
                        pe.wait_ge(gelu_done, 2 * k + n - 1)
                    for c in range(FC // 2):
                        ins = pe.transpose(bank[4 + n][:, c * 128:(c + 1) * 128],
                                           hid[:, par, (4 * n + c) * 128:(4 * n + c + 1) * 128], ident[:, :])
                    ins.then_inc(hidT_ps, 1)

            def down(k, par):
                e = pe.value_load(blk_ex[0:1, bass.ds(k, 1)], min_val=0, max_val=X - 1)
                if not early(k, 1):
                    pe.wait_ge(y_biased, k)
                for c in range(FC):
                    if c % 4 == 0:
                        pe.wait_ge(gelu_done, 2 * k + c // 4 + 1)
                    ins = pe.matmul(bank[7][:, 0:E], actT[:, par, c, :], w2_sb[:, bass.ds(e, 1), c, :],
                                    start=(c == 0), stop=(c == FC - 1))
                ins.then_inc(y_ps, 1)

            def turn(k, slot, more=True):
                par = slot % 2
                hidden_T(k, par)
                hidden(k + 1, 1 - par)
                if more:
                    block_T(k + 2, (slot + 2) % RING)
                down(k, par)

            block_T(0, 0)
            hidden(0, 0)
            block_T(1, 1)
            loop_by(RING, pe, NBLK - 2, turn)
            turn(NBLK - 2, 0, more=False)
            hidden_T(NBLK - 1, 1)
            down(NBLK - 1, 1)

        @block.vector
        def _(dve):
            dve.wait_ge(pool_const, 14)
            dve.tensor_scalar(part_bit[:, :], part_no[:, :], DK, None, ALU.bitwise_and).then_inc(dve_chain, 1)
            dve.wait_ge(dve_chain, 1)
            dve.tensor_scalar(parity_of[:, 0:1], part_bit[:, :], 0.0, None, ALU.is_equal)
            dve.tensor_scalar(parity_of[:, 1:2], part_bit[:, :], 0.0, None, ALU.is_gt).then_inc(dve_const, 1)
            dve.wait_ge(ld_cls, 32)
            dve.tensor_tensor(cls_pos[:, 0, :], cls_pos[:, 0, :], cls_pos[:, 1, :], ALU.add).then_inc(cls_done, 1)

            patches = px.rearrange("r c (p w q) -> r c w p q", p=PS, w=G)

            def patch_stats(w):
                for c in range(C):
                    if w == 0:
                        dve.wait_ge(ld_x[c], 16)
                    ins = dve.bn_stats(px_six[:, w, c, :], patches[:, c, w])
                ins.then_inc(p_chain, 1)
                dve.wait_ge(p_chain, w + 1)
                dve.bn_aggr(pmv[:, w, :], px_six[:, w, :, :]).then_inc(px_stats, 1)

            def patch_norm(w):
                dve.wait_ge(px_rstd, w + 1)
                if w >= 2:
                    dve.wait_ge(px_T, w - 1)
                dve.tensor_scalar(pxn[:, w % 2, :].rearrange("r (c p q) -> r c p q", c=C, p=PS),
                                  patches[:, :, w], prs[:, w, 0:1], prs[:, w, 1:2],
                                  ALU.mult, ALU.subtract).then_inc(px_norm, 1)

            def proj_stats(w):
                dve.wait_ge(pz_ps, w + 1)
                if w >= 2:
                    dve.wait_ge(st_patch[w % 2], 16 * (w // 2))
                dve.tensor_tensor(pz[:, w % 2, :], bank[4 + w % 2][0:R, 0:E], b_patch_bc, ALU.add)\
                   .then_inc(pz_biased, 1)
                dve.wait_ge(pz_biased, w + 1)
                dve.bn_stats(pz_six[:, w, :], pz[:, w % 2, :]).then_inc(pz_chain, 1)
                dve.wait_ge(pz_chain, 3 * w + 1)
                dve.bn_aggr(zmv[:, w, :], pz_six[:, w, :]).then_inc(pz_stats, 1)

            def proj_norm(w):
                z = pz[:, w % 2, :]
                dve.wait_ge(pz_rstd, w + 1)
                dve.tensor_scalar(z, z, zrs[:, w, 0:1], zrs[:, w, 1:2], ALU.mult, ALU.subtract).then_inc(pz_chain, 1)
                dve.wait_ge(pz_chain, 3 * w + 2)
                dve.tensor_tensor(z, z, ln2_g_bc, ALU.mult).then_inc(pz_chain, 1)
                dve.wait_ge(pz_chain, 3 * w + 3)
                dve.tensor_tensor(z, z, pos_bc[:, w, :], ALU.add).then_inc(pz_done, 1)

            patch_stats(0)
            dve.wait_ge(posb_done, 1)
            for w in range(G + 2):
                if w + 1 < G:
                    patch_stats(w + 1)
                if w < G:
                    patch_norm(w)
                if w >= 2:
                    proj_stats(w - 2)
                    proj_norm(w - 2)

            dve.wait_ge(ld_txt, 32)
            dve.wait_ge(ld_tok, 16)
            for n, entries in enumerate(LN1_GROUPS):
                for b in entries:
                    ins = dve.bn_stats(six1[:, b, :], rows[:, b, RES:RES + E])
                ins.then_inc(ln1_chain, 1)
                dve.wait_ge(ln1_chain, n + 1)
                for b in entries:
                    ins = dve.bn_aggr(mv1[:, b, :], six1[:, b, :])
                ins.then_inc(ln1_stats, 1)

            def attention(f, b, r, par):
                A, BB = bank[0], bank[1]
                if b is not None:
                    ov = A[0:T, 0:H * (DK + 1)].rearrange("p (h d) -> p h d", h=H)
                    dve.wait_ge(pv_ps, b + 1)
                    dve.reciprocal(rsum[:, :], ov[:, :, DK]).then_inc(rsum_done, 1)
                    dve.wait_ge(rsum_done, b + 1)
                    if not early(b, 1):
                        dve.wait_ge(oT_ps, b)
                    dve.tensor_tensor(o_sb.rearrange("p (h d) -> p h d", h=H), ov[:, :, 0:DK],
                                      rsum[:, :].unsqueeze(2).to_broadcast([T, H, DK]), ALU.mult)\
                       .then_inc(o_done, 1)
                if f is not None:
                    for g in range(NG):
                        sv = bank[2 + g][0:T, 0:HG * T].rearrange("p (h t) -> p h t", h=HG)
                        mx = smax[:, par, HG * g:HG * (g + 1)]
                        dve.wait_ge(scores_ps, NG * f + g + 1)
                        dve.tensor_reduce(mx, sv, AX.X, ALU.max).then_inc(max_done, 1)
                        dve.wait_ge(max_done, NG * f + g + 1)
                        if not early(f, 2):
                            dve.wait_ge(pT_ps, NG * (f - 2) + g + 1)
                        dve.tensor_tensor(probs[:, par, HG * g:HG * (g + 1), :], sv,
                                          mx.unsqueeze(2).to_broadcast([T, HG, T]), ALU.subtract)\
                           .then_inc(shifted, 1)
                if b is not None:
                    res = x2[:, par, RES:RES + E]
                    dve.wait_ge(proj_ps, b + 1)
                    if not early(b, 2):
                        dve.wait_ge(x2_kept, b - 1)
                    dve.tensor_tensor(res, BB[0:T, 0:E], rows[:, b, RES:RES + E], ALU.add).then_inc(resid_done, 1)
                    dve.wait_ge(resid_done, b + 1)
                    dve.bn_stats(six2[:, par, :], res).then_inc(ln2_chain, 1)
                if r is not None:
                    dve.wait_ge(logit_ps, r + 1)
                    if b is not None:
                        dve.wait_ge(ln2_chain, b + 1)
                    dve.tensor_copy(logits[:, r, :], A[0:T, 0:X]).then_inc(logit_kept, 1)
                elif b is not None:
                    dve.wait_ge(ln2_chain, b + 1)
                if b is not None:
                    dve.bn_aggr(mv2[:, par, :], six2[:, par, :]).then_inc(ln2_stats, 1)

            attention_steps(dve, attention)

            steps = [0]

            def then(ins):
                steps[0] += 1
                ins.then_inc(r_chain, 1)
                dve.wait_ge(r_chain, steps[0])

            over_x = lambda v: v.unsqueeze(2).to_broadcast([T, B, X])
            over_b = lambda v: v.unsqueeze(1).to_broadcast([T, B, X])
            dve.wait_ge(logit_kept, B)
            then(dve.tensor_reduce(lmax[:, :], logits[:, :, :], AX.X, ALU.max))
            dve.tensor_tensor(lexp[:, :, :], logits[:, :, :], over_x(lmax[:, :]), ALU.subtract)\
               .then_inc(l_shifted, 1)
            then(dve.tensor_tensor(lkey[:, :, :], logits[:, :, :], over_x(lmax[:, :]), ALU.is_equal))
            then(dve.scalar_tensor_tensor(out=lkey[:, :, :], in0=lkey[:, :, :], scalar=float(-X),
                                          in1=over_b(expert_no[:, :]), op0=ALU.mult, op1=ALU.add))
            then(dve.tensor_reduce(lfirst[:, :], lkey[:, :, :], AX.X, ALU.min))
            then(dve.tensor_tensor(chosen[:, :, :], lkey[:, :, :], over_x(lfirst[:, :]), ALU.is_equal))
            dve.tensor_copy(chosen_bf[:, :, :], chosen[:, :, :]).then_inc(chosen_done, 1)
            dve.wait_ge(rank_ps, 1)
            then(dve.tensor_reduce(count[:, :], bank[1][0:T, 0:B * X].rearrange("p (b x) -> p x b", b=B),
                                   AX.X, ALU.add))
            then(dve.tensor_tensor(many[:, :, :], count[:, :].unsqueeze(2).to_broadcast([T, X, NFULL]),
                                   filled[:, :].unsqueeze(1).to_broadcast([T, X, NFULL]), ALU.is_gt))
            then(dve.tensor_reduce(nblk[:, :], many[:, :, :], AX.X, ALU.add))
            then(dve.tensor_tensor_scan(blk_end[:, :], ones_f[:, :], nblk[:, :], 0.0, ALU.mult, ALU.add))
            then(dve.tensor_tensor(start[:, :], blk_end[:, :], nblk[:, :], ALU.subtract))
            then(dve.tensor_scalar(start[:, :], start[:, :], float(SLOT), None, ALU.mult))
            then(dve.tensor_tensor(slot_of[:, :, :], bank[0][0:T, 0:B * X].rearrange("p (b x) -> p b x", b=B),
                                   over_b(start[:, :]), ALU.add))
            then(dve.tensor_tensor(slot_of[:, :, :], slot_of[:, :, :], chosen[:, :, :], ALU.mult))
            then(dve.tensor_reduce(pos_f[:, :], slot_of[:, :, :], AX.X, ALU.add))
            dve.tensor_copy(pos[:, :], pos_f[:, :]).then_inc(pos_done, 1)
            dve.wait_ge(l_exp, 1)
            then(dve.tensor_reduce(lsum[:, :], lexp[:, :, :], AX.X, ALU.add))
            dve.reciprocal(rows[:, :, WGT], lsum[:, :]).then_inc(weight_done, 1)
            then(dve.tensor_tensor(blk_cmp[:, :, :], blk_no[:, :].unsqueeze(2).to_broadcast([1, NBLK, X]),
                                   blk_end[0:1, :].unsqueeze(1).to_broadcast([1, NBLK, X]), ALU.is_ge))
            then(dve.tensor_reduce(blk_ex_f[:, :], blk_cmp[:, :, :], AX.X, ALU.add))
            dve.tensor_scalar(blk_ex[:, :], blk_ex_f[:, :], float(X - 1), None, ALU.min).then_inc(blk_ex_done, 1)
            dve.wait_ge(blk_ex_done, 1)
            dve.wait_ge(ld_b2, 16)

            def copy_block(k, par):
                dve.wait_ge(blkT_ps, k + 1)
                if not early(k, 2):
                    dve.wait_ge(hid_ps, 2 * (k - 1))
                dve.tensor_copy(blkT[:, par, :, :], bank[6][:, 0:E].rearrange("p (c t) -> p c t", c=EC))\
                   .then_inc(blkT_copied, 1)

            def copy_hidden(k, par):
                for n in range(2):
                    dve.wait_ge(hid_ps, 2 * k + n + 1)
                    if not early(k, 2):
                        dve.wait_ge(hidT_ps, 2 * (k - 2) + n + 1)
                    dve.tensor_copy(hid[:, par, n * 512:(n + 1) * 512], bank[2 * par + n][:, :])\
                       .then_inc(hid_copied, 1)

            def finish_block(k, slot):
                par = slot % 2
                e = dve.value_load(blk_ex[0:1, bass.ds(k, 1)], min_val=0, max_val=X - 1)
                y = blk_out[:, par, :]
                dve.wait_ge(y_ps, k + 1)
                if not early(k, 2):
                    dve.wait_ge(st_out[par], 8 * (k - par))
                dve.tensor_tensor(y, bank[7][:, 0:E], b2_bc[:, e, :], ALU.add).then_inc(y_biased, 1)
                dve.wait_ge(y_biased, k + 1)
                dve.wait_ge(ld_blk[slot], 16 // RING * (k - slot) + 16)
                dve.scalar_tensor_tensor(out=y, in0=y, scalar=blk_in[:, slot, WGT:WGT + 1],
                                         in1=blk_in[:, slot, RES:RES + E], op0=ALU.mult, op1=ALU.add)\
                   .then_inc(blk_done, 1)

            def turn(k, slot, more=True):
                copy_hidden(k + 1, 1 - slot % 2)
                if more:
                    copy_block(k + 2, slot % 2)
                finish_block(k, slot)

            copy_block(0, 0)
            copy_hidden(0, 0)
            copy_block(1, 1)
            loop_by(RING, dve, NBLK - 2, turn)
            turn(NBLK - 2, (NBLK - 2) % RING, more=False)
            finish_block(NBLK - 1, (NBLK - 1) % RING)


_INS = ["x", "txt", "L0_tok_ln1_g", "L0_tok_ln1_b", "L0_tok_W_proj", "L0_tok_b_proj", "L0_tok_ln2_g",
        "L0_tok_ln2_b", "L0_tok_cls_token", "L0_tok_pos_emb", "L0_attn_w_attn", "L0_attn_w_proj",
        "L0_ffn_gate_w", "L0_ffn_w1", "L0_ffn_b1", "L0_ffn_w2", "L0_ffn_b2"]


def kernel(**inputs):
    import numpy as _np
    import concourse.bacc as _bacc
    from concourse import mybir as _mybir
    from concourse.bass_utils import run_bass_kernel_spmd as _run

    nc = _bacc.Bacc("TRN2", target_bir_lowering=False, num_devices=1)
    arrays, args = {}, []
    for name in _INS:
        a = _np.ascontiguousarray(inputs[name])
        arrays[f"in_{name}_dram"] = a
        args.append(nc.dram_tensor(f"in_{name}_dram", a.shape, _mybir.dt.from_np(a.dtype),
                                   kind="ExternalInput").ap())
    images, _, _, _ = inputs["x"].shape
    tokens = inputs["L0_tok_pos_emb"].shape[1] + inputs["txt"].shape[1]
    shape = (images, tokens, inputs["txt"].shape[2])
    args.append(nc.dram_tensor("out_0_dram", shape, _mybir.dt.float32, kind="ExternalOutput").ap())
    fusion_program(nc, *args)
    r = _run(nc, [arrays], core_ids=[0])
    return r.results[0]["out_0_dram"]
```

```python
from contextlib import ExitStack

import concourse.bass as bass
from concourse import mybir

ALU = mybir.AluOpType
ACT = mybir.ActivationFunctionType
AX = mybir.AxisListType
F32 = mybir.dt.float32
BF16 = mybir.dt.bfloat16
I32 = mybir.dt.int32
U32 = mybir.dt.uint32
LN_EPS = 1e-5
MASKED = -1e30


def loop_by(unroll, eng, count, step):
    rest = count % unroll
    for n in range(unroll + rest):
        step(n, n % unroll)
    with eng.Fori(1, count // unroll) as i:
        for n in range(rest, rest + unroll):
            step(unroll * i + n, n % unroll)


def fusion_program(nc, x, txt, ln1_g, ln1_b, w_patch, b_patch, ln2_g, ln2_b, cls_token, pos_emb,
                   w_attn, w_proj, gate_w, w1, b1, w2, b2, out):
    B, C, HH, _ = x.shape
    S, E = txt.shape[1:]
    PS = 16
    G = HH // PS
    T = 1 + G * G + S
    R = B * G
    PD = C * PS * PS
    PC = PD // 128
    EC = E // 128
    H, DK = 16, E // 16
    X, _, F = w1.shape
    FC = F // 128
    SLOT = 128
    NBLK = (B * T + X * (SLOT - 1)) // SLOT
    NBLK += NBLK % 2
    NFULL = -(-B * T // SLOT)
    RES, WGT, TOK, ROW = E, 2 * E, 2 * E + 1, 2 * E + 4
    NOBODY = 1 << 20
    RING = 4
    HG = 4
    NG = H // HG

    sorted_rows = nc.dram_tensor("sorted_rows", [NBLK * SLOT, ROW], F32)
    patch_rows = nc.dram_tensor("patch_rows", [R, G, E], F32)
    out_rows = out.rearrange("b t d -> (b t) d")

    with ExitStack() as ctx:
        def sb(name, shape, dt=F32):
            return ctx.enter_context(nc.sbuf_tensor(name, shape, dt))

        def sem(name):
            return ctx.enter_context(nc.semaphore(name))

        experts = sb("experts", [128, X, EC * F + FC * E])
        w1_sb = experts[:, :, 0:EC * F].rearrange("p e (k f) -> p e k f", k=EC)
        w2_sb = experts[:, :, EC * F:].rearrange("p e (c d) -> p e c d", c=FC)
        rows = sb("rows", [T, B, ROW])

        def carver(room):
            taken = [0]

            def carve(width):
                taken[0] += width
                assert taken[0] <= room.shape[1]
                return room[:, taken[0] - width:taken[0]]
            return carve

        carve = carver(experts[:, X - 4:X - 1, :].rearrange("p e n -> p (e n)"))
        px = carve(C * PS * HH).rearrange("p (c n) -> p c n", c=C)[0:R]
        pxn = carve(2 * PD).rearrange("p (s n) -> p s n", s=2)[0:R]
        w_patch_sb = carve(PC * E).rearrange("p (c e) -> p c e", c=PC)
        w_nat = carve(4 * EC * E).rearrange("p (n e) -> p n e", n=4 * EC)
        b1_nat = carve(128)[0:X * FC]
        probs = experts[:, X - 1, 0:2 * H * T].rearrange("p (s h t) -> p s h t", s=2, h=H)[0:T]

        WORK = 7184
        work = sb("work", [128, WORK])
        carve = carver(work[:, :])
        pxT = carve(2 * PC * R).rearrange("p (s c r) -> p s c r", s=2, c=PC)
        pz = carve(2 * E).rearrange("p (s n) -> p s n", s=2)[0:R]
        b_patch_bc = carve(E)[0:R]
        ln2_g_bc = carve(E)[0:R]
        ln2_b_bc = carve(E)[0:R]
        pos_bc = carve(G * E).rearrange("p (w n) -> p w n", w=G)[0:R]
        cls_pos = carve(2 * E).rearrange("p (s n) -> p s n", s=2)[0:1]
        carve = carver(work[:, :])
        probsT = carve(H * T).rearrange("p (h t) -> p h t", h=H)[0:T]
        xn = carve(2 * E).rearrange("p (s n) -> p s n", s=2)[0:T]
        xnT = carve(2 * EC * T).rearrange("p (s k t) -> p s k t", s=2, k=EC)
        qT = carve(EC * T).rearrange("p (k t) -> p k t", k=EC)
        k_heads = carve(H * T).rearrange("p (k h t) -> p k h t", k=EC, h=H // EC)
        v_aug = carve(2 * H * (DK + 1)).rearrange("p (s h d) -> p s h d", s=2, h=H)[0:T]
        o_sb = carve(E)[0:T]
        oT = carve(EC * T).rearrange("p (k t) -> p k t", k=EC)
        x2 = carve(4 * E).rearrange("p (s n) -> p s n", s=2)[0:T]
        x2T = carve(EC * T).rearrange("p (k t) -> p k t", k=EC)
        carve = carver(work[:, :])
        hid = carve(2 * F).rearrange("p (s n) -> p s n", s=2)
        actT = carve(2 * F).rearrange("p (s c t) -> p s c t", s=2, c=FC)
        blk_out = carve(2 * E).rearrange("p (s n) -> p s n", s=2)
        blkT = carve(2 * E).rearrange("p (s c t) -> p s c t", s=2, c=EC)
        blk_in = carve(RING * ROW).rearrange("p (s n) -> p s n", s=RING)

        attn_w = sb("attn_w", [128, EC * 3 * E + EC * E])
        w_attnT = attn_w[:, 0:EC * 3 * E].rearrange("p (k n) -> p k n", k=EC)
        w_projT = attn_w[:, EC * 3 * E:].rearrange("p (k n) -> p k n", k=EC)
        b2_bc = attn_w[:, 0:X * E].rearrange("p (x e) -> p x e", x=X)

        gate_sb = sb("gate_sb", [128, EC, X])
        b1T = sb("b1T", [128, X * FC])
        ident = sb("ident", [128, 128])
        ident_bf = sb("ident_bf", [T, T], BF16)
        mask_bf = sb("mask_bf", [T, HG, T], BF16)
        before = sb("before", [T, T], BF16)
        ones_bf = sb("ones_bf", [T, T], BF16)
        head_of = sb("head_of", [128, H // EC])
        minus_half = sb("minus_half", [128, B])
        eps = sb("eps", [128, B])
        pg = sb("pg", [128, 2, C, PC // C])
        px_six = sb("px_six", [R, G, C, 6])
        pz_six = sb("pz_six", [R, G, 6])
        pmv = sb("pmv", [R, G, 2])
        prs = sb("prs", [R, G, 2])
        zmv = sb("zmv", [R, G, 2])
        zrs = sb("zrs", [R, G, 2])
        six1 = sb("six1", [T, B, 6])
        six2 = sb("six2", [T, 2, 6])
        mv1 = sb("mv1", [T, B, 2])
        rs1 = sb("rs1", [T, B, 2])
        mv2 = sb("mv2", [T, 2, 2])
        rs2 = sb("rs2", [T, 2, 2])
        smax = sb("smax", [T, 2, H])
        rsum = sb("rsum", [T, H])
        logits = sb("logits", [T, B, X])
        lmax = sb("lmax", [T, B])
        lexp = sb("lexp", [T, B, X])
        lsum = sb("lsum", [T, B])
        lkey = sb("lkey", [T, B, X])
        lfirst = sb("lfirst", [T, B])
        chosen = sb("chosen", [T, B, X])
        chosen_bf = sb("chosen_bf", [T, B, X], BF16)
        expert_no = sb("expert_no", [T, X])
        filled = sb("filled", [T, NFULL])
        many = sb("many", [T, X, NFULL])
        count = sb("count", [T, X])
        nblk = sb("nblk", [T, X])
        blk_end = sb("blk_end", [T, X])
        start = sb("start", [T, X])
        slot_of = sb("slot_of", [T, B, X])
        pos_f = sb("pos_f", [T, B])
        pos = sb("pos", [T, B], I32)
        blk_no = sb("blk_no", [1, NBLK])
        blk_cmp = sb("blk_cmp", [1, NBLK, X])
        blk_ex_f = sb("blk_ex_f", [1, NBLK])
        blk_ex = sb("blk_ex", [1, NBLK], I32)
        empty_row = sb("empty_row", [128, ROW])
        ones_f = sb("ones_f", [T, X])

        bank = [ctx.enter_context(nc.psum_tensor(f"bank{i}", [128, 512], F32)) for i in range(8)]

        ld_x = [sem(f"ld_x{c}") for c in range(C)]
        ld_patch = sem("ld_patch")
        ld_z = sem("ld_z")
        ld_const = sem("ld_const")
        ld_nat = sem("ld_nat")
        ld_cls = sem("ld_cls")
        ld_txt = sem("ld_txt")
        ld_tok = sem("ld_tok")
        ld_w = [sem(f"ld_w{e}") for e in range(X)]
        st_patch = [sem("st_patch0"), sem("st_patch1")]
        st_empty = sem("st_empty")
        st_rows = sem("st_rows")
        ld_blk = [sem(f"ld_blk{s}") for s in range(RING)]
        ld_b2 = sem("ld_b2")
        st_out = [sem("st_out0"), sem("st_out1")]
        pool_const = sem("pool_const")
        pool_chain = sem("pool_chain")
        cls_done = sem("cls_done")
        v_ones = sem("v_ones")
        px_stats = sem("px_stats")
        px_rstd = sem("px_rstd")
        px_norm = sem("px_norm")
        px_T = sem("px_T")
        px_Tcopied = sem("px_Tcopied")
        pz_ps = sem("pz_ps")
        pz_biased = sem("pz_biased")
        pz_stats = sem("pz_stats")
        pz_rstd = sem("pz_rstd")
        pz_normed = sem("pz_normed")
        pz_scaled = sem("pz_scaled")
        pz_done = sem("pz_done")
        px_pool = sem("px_pool")
        pz_pool = sem("pz_pool")
        p_chain = sem("p_chain")
        pz_chain = sem("pz_chain")
        posb_done = sem("posb_done")
        wT_ps = sem("wT_ps")
        wT_copied = sem("wT_copied")
        ln1_chain = sem("ln1_chain")
        ln1_stats = sem("ln1_stats")
        ln1_pool = sem("ln1_pool")
        xn_scaled = sem("xn_scaled")
        xn_ready = sem("xn_ready")
        xnT_ps = sem("xnT_ps")
        xnT_copied = sem("xnT_copied")
        qk_ps = sem("qk_ps")
        q_copied = sem("q_copied")
        k_copied = sem("k_copied")
        v_ps = sem("v_ps")
        v_copied = sem("v_copied")
        scores_ps = sem("scores_ps")
        max_done = sem("max_done")
        shifted = sem("shifted")
        exp_done = sem("exp_done")
        pT_ps = sem("pT_ps")
        pT_copied = sem("pT_copied")
        pv_ps = sem("pv_ps")
        rsum_done = sem("rsum_done")
        o_done = sem("o_done")
        oT_ps = sem("oT_ps")
        oT_copied = sem("oT_copied")
        proj_ps = sem("proj_ps")
        resid_done = sem("resid_done")
        ln2_chain = sem("ln2_chain")
        ln2_stats = sem("ln2_stats")
        ln2_pool = sem("ln2_pool")
        x2n_ready = sem("x2n_ready")
        x2_kept = sem("x2_kept")
        x2T_ps = sem("x2T_ps")
        x2T_copied = sem("x2T_copied")
        logit_ps = sem("logit_ps")
        logit_kept = sem("logit_kept")
        r_chain = sem("r_chain")
        l_shifted = sem("l_shifted")
        l_exp = sem("l_exp")
        chosen_done = sem("chosen_done")
        rank_ps = sem("rank_ps")
        pos_done = sem("pos_done")
        weight_done = sem("weight_done")
        blk_ex_done = sem("blk_ex_done")
        blkT_ps = sem("blkT_ps")
        blkT_copied = sem("blkT_copied")
        hid_ps = sem("hid_ps")
        hid_copied = sem("hid_copied")
        hidT_ps = sem("hidT_ps")
        gelu_done = sem("gelu_done")
        y_ps = sem("y_ps")
        y_biased = sem("y_biased")
        blk_done = sem("blk_done")

        LN1_GROUPS = (range(0, 2), range(2, B))

        PATCH_LOADS = 16 * 3 * (PC // C)

        def attention_steps(eng, step):
            for s in range(4):
                step(s, s % 2)
            with eng.Fori(2, B // 2 - 1) as i:
                step(2 * i, 0)
                step(2 * i + 1, 1)
            for s in range(B - 2, B + 3):
                step(s, s % 2)

        def entry(n):
            return n if not isinstance(n, int) or 0 <= n < B else None

        def early(index, least):
            return isinstance(index, int) and index < least

        block = ctx.enter_context(nc.Block())

        @block.sync
        def _(sp):
            xv = x.rearrange("b c (h p) w -> c b h (p w)", p=PS)
            for c in range(C):
                sp.dma_start(px[:, c, :], xv[c]).then_inc(ld_x[c], 16)
            sp.dma_start(rows[T - S:T, :, RES:RES + E], txt.rearrange("b s e -> s b e")).then_inc(ld_txt, 16)
            sp.wait_ge(cls_done, 1)
            sp.dma_start(rows[0:1, :, RES:RES + E], cls_pos[:, 0:1, :].to_broadcast([1, B, E])).then_inc(ld_txt, 16)
            for w in range(G):
                sp.wait_ge(pz_done, w + 1)
                sp.dma_start(patch_rows[:, w, :], pz[:, w % 2, :]).then_inc(st_patch[w % 2], 16)
            for par in range(2):
                sp.wait_ge(st_patch[par], 8 * G)
            sp.dma_start(rows[1:1 + G * G, :, RES:RES + E],
                         patch_rows.rearrange("(b h) w e -> (h w) b e", b=B)).then_inc(ld_tok, 16)
            sp.wait_ge(wT_copied, 4 * EC + 1)
            for e in range(X - 1):
                sp.dma_start(w1_sb[:, e], w1[e].rearrange("(k p) f -> p k f", p=128)).then_inc(ld_w[e], 16)
                sp.dma_start(w2_sb[:, e], w2[e].rearrange("(c p) d -> p c d", p=128)).then_inc(ld_w[e], 16)
            sp.wait_ge(pool_const, 14)
            sp.dma_start(sorted_rows.rearrange("(k p) n -> p k n", p=SLOT),
                         empty_row[:, :].unsqueeze(1).to_broadcast([SLOT, NBLK, ROW])).then_inc(st_empty, 16)
            sp.wait_ge(pT_ps, NG * B)
            sp.dma_start(w1_sb[:, X - 1], w1[X - 1].rearrange("(k p) f -> p k f", p=128)).then_inc(ld_w[X - 1], 16)
            sp.dma_start(w2_sb[:, X - 1], w2[X - 1].rearrange("(c p) d -> p c d", p=128)).then_inc(ld_w[X - 1], 16)
            sp.wait_ge(proj_ps, B)
            sp.dma_start(b2_bc, b2.partition_broadcast(128)).then_inc(ld_b2, 16)

            def load_block(k, slot):
                if not early(k, RING):
                    sp.wait_ge(st_out[slot % 2], 8 * (k - RING - slot % 2) + 16)
                sp.dma_start(blk_in[:, slot, :], sorted_rows[bass.ds(k * SLOT, SLOT), :]).then_inc(ld_blk[slot], 16)

            sp.wait_ge(st_rows, 16 * B)
            loop_by(RING, sp, NBLK, load_block)

        @block.gpsimd
        def _(pool):
            pool.memset(ident[:, :], 0.0).then_inc(pool_chain, 1)
            pool.memset(ident_bf[:, :], 0.0).then_inc(pool_chain, 1)
            pool.memset(mask_bf[:, :, :], 0.0).then_inc(pool_chain, 1)
            pool.memset(before[:, :], 1.0).then_inc(pool_chain, 1)
            pool.memset(ones_bf[:, :], 1.0).then_inc(pool_const, 1)
            pool.memset(ones_f[:, :], 1.0).then_inc(pool_const, 1)
            pool.memset(minus_half[:, :], -0.5)
            pool.memset(eps[:, :], LN_EPS).then_inc(pool_const, 1)
            pool.memset(empty_row[:, :], 0.0).then_inc(pool_chain, 1)
            pool.memset(head_of[:, :], 1.0).then_inc(pool_chain, 1)
            pool.wait_ge(pool_chain, 6)
            pool.affine_select(out=ident[:, :], in_=ident[:, :], compare_op=ALU.not_equal, fill=1.0,
                               base=0, pattern=[[-1, 128]], channel_multiplier=1).then_inc(pool_const, 1)
            pool.affine_select(out=ident_bf[:, :], in_=ident_bf[:, :], compare_op=ALU.not_equal, fill=1.0,
                               base=0, pattern=[[-1, T]], channel_multiplier=1).then_inc(pool_const, 1)
            pool.affine_select(out=mask_bf[:, :, :], in_=mask_bf[:, :, :], compare_op=ALU.is_ge, fill=MASKED,
                               base=0, pattern=[[0, HG], [-1, T]], channel_multiplier=1).then_inc(pool_const, 1)
            pool.affine_select(out=before[:, :], in_=before[:, :], compare_op=ALU.is_gt, fill=0.0,
                               base=0, pattern=[[1, T]], channel_multiplier=-1).then_inc(pool_const, 1)
            pool.affine_select(out=head_of[:, :], in_=head_of[:, :], compare_op=ALU.is_ge, fill=0.0,
                               base=0, pattern=[[-DK, H // EC]], channel_multiplier=1).then_inc(pool_chain, 1)
            pool.wait_ge(pool_chain, 7)
            pool.affine_select(out=head_of[:, :], in_=head_of[:, :], compare_op=ALU.is_ge, fill=0.0,
                               base=DK - 1, pattern=[[DK, H // EC]], channel_multiplier=-1).then_inc(pool_const, 1)
            pool.iota(expert_no[:, :], pattern=[[1, X]], base=0, channel_multiplier=0,
                      allow_small_or_imprecise_dtypes=True).then_inc(pool_const, 1)
            pool.iota(filled[:, :], pattern=[[SLOT, NFULL]], base=0, channel_multiplier=0,
                      allow_small_or_imprecise_dtypes=True).then_inc(pool_const, 1)
            pool.iota(blk_no[:, :], pattern=[[1, NBLK]], base=0, channel_multiplier=0,
                      allow_small_or_imprecise_dtypes=True).then_inc(pool_const, 1)
            pool.iota(rows[:, :, TOK].bitcast(I32), pattern=[[T, B]], base=0, channel_multiplier=1)\
                .then_inc(pool_const, 1)
            pool.iota(empty_row[:, TOK:TOK + 1].bitcast(I32), pattern=[[0, 1]], base=NOBODY,
                      channel_multiplier=0).then_inc(pool_const, 1)
            pool.memset(rows[:, :, TOK + 1:ROW], 0.0).then_inc(pool_const, 1)
            def rstd(mv, rs, chain, base):
                n, m, _ = mv.shape
                pool.tensor_tensor(rs[:, :, 1], mv[:, :, 1], eps[0:n, 0:m], ALU.add).then_inc(chain, 1)
                pool.wait_ge(chain, base + 1)
                pool.tensor_tensor(rs[:, :, 0], rs[:, :, 1], minus_half[0:n, 0:m], ALU.pow).then_inc(chain, 1)
                pool.wait_ge(chain, base + 2)
                return pool.tensor_tensor(rs[:, :, 1], mv[:, :, 0], rs[:, :, 0], ALU.mult)

            for w in range(G + 2):
                if w < G:
                    pool.wait_ge(px_stats, w + 1)
                    rstd(pmv[:, w:w + 1, :], prs[:, w:w + 1, :], px_pool, 2 * w).then_inc(px_rstd, 1)
                if w == 1:
                    pool.wait_ge(ld_z, 16 * 4)
                    for v in range(G):
                        ins = pool.tensor_tensor(pos_bc[:, v, :], pos_bc[:, v, :], ln2_b_bc, ALU.add)
                    ins.then_inc(posb_done, 1)
                if w >= 2:
                    pool.wait_ge(pz_stats, w - 1)
                    rstd(zmv[:, w - 2:w - 1, :], zrs[:, w - 2:w - 1, :], pz_pool, 2 * (w - 2)).then_inc(pz_rstd, 1)
            for par in range(2):
                pool.wait_ge(st_patch[par], 8 * G)
            pool.wait_ge(ld_txt, 32)
            pool.memset(v_aug[:, :, :, :], 1.0).then_inc(v_ones, 1)

            def ln1_rstd(n):
                g = slice(LN1_GROUPS[n].start, LN1_GROUPS[n].stop)
                pool.wait_ge(ln1_stats, n + 1)
                rstd(mv1[:, g, :], rs1[:, g, :], ln1_pool, 3 * n).then_inc(ln1_pool, 1)
                pool.wait_ge(ln1_pool, 3 * n + 3)

            def normalise(n, par):
                pool.tensor_tensor(xn[:, par, :], rows[:, n, RES:RES + E],
                                   rs1[:, n, 0:1].to_broadcast([T, E]), ALU.mult).then_inc(xn_scaled, 1)
                pool.wait_ge(xn_scaled, n + 1)
                pool.tensor_tensor(xn[:, par, :], xn[:, par, :],
                                   rs1[:, n, 1:2].to_broadcast([T, E]), ALU.subtract).then_inc(xn_ready, 1)

            ln1_rstd(0)
            normalise(0, 0)
            normalise(1, 1)
            ln1_rstd(1)

            def attention(s, par):
                ahead, b = entry(s + 2), entry(s - 2)
                if ahead is not None:
                    pool.wait_ge(xnT_ps, s + 1)
                    normalise(ahead, par)
                if b is not None:
                    pool.wait_ge(ln2_stats, b + 1)
                    rstd(mv2[:, par:par + 1, :], rs2[:, par:par + 1, :], ln2_pool, 4 * b).then_inc(ln2_pool, 1)
                    pool.wait_ge(ln2_pool, 4 * b + 3)
                    if not early(b, 2):
                        pool.wait_ge(x2T_ps, b - 1)
                    pool.tensor_tensor(x2[:, par, 0:E], x2[:, par, RES:RES + E],
                                       rs2[:, par, 0:1].to_broadcast([T, E]), ALU.mult).then_inc(ln2_pool, 1)
                    pool.wait_ge(ln2_pool, 4 * b + 4)
                    pool.tensor_tensor(x2[:, par, 0:E], x2[:, par, 0:E],
                                       rs2[:, par, 1:2].to_broadcast([T, E]), ALU.subtract).then_inc(x2n_ready, 1)
                    pool.wait_ge(x2n_ready, b + 1)
                    pool.tensor_copy(rows[:, b, 0:2 * E], x2[:, par, :]).then_inc(x2_kept, 1)

            attention_steps(pool, attention)

            pool.wait_ge(st_empty, 16)
            pool.wait_ge(x2_kept, B)
            pool.wait_ge(resid_done, B)
            pool.wait_ge(weight_done, 1)
            pool.wait_ge(pos_done, 1)
            for b in range(B):
                pool.indirect_dma_start(
                    out=sorted_rows[:, :], out_offset=bass.IndirectOffsetOnAxis(ap=pos[:, b:b + 1].bitcast(U32), axis=0),
                    in_=rows[:, b, :], in_offset=None).then_inc(st_rows, 16)

            last_row = pool.to_reg(B * T - 1)

            def store_block(k, par):
                pool.wait_ge(blk_done, k + 1)
                pool.indirect_dma_start(
                    out=out_rows, out_offset=bass.IndirectOffsetOnAxis(
                        ap=blk_in[:, k % RING, TOK:TOK + 1].bitcast(U32), axis=0),
                    in_=blk_out[:, par, :], in_offset=None,
                    bounds_check=last_row, oob_is_err=False).then_inc(st_out[par], 16)

            for k in range(NBLK):
                store_block(k, k % 2)
            for par in range(2):
                pool.wait_ge(st_out[par], 16 * (NBLK // 2))

        @block.scalar
        def _(act):
            for u in range(PC // C):
                act.dma_start(w_patch_sb.rearrange("k (c u) e -> k u c e", c=C)[:, u],
                              w_patch.rearrange("(u k c) e -> u k c e", u=PC // C, c=C)[u]).then_inc(ld_patch, 16)
            with nc.allow_non_contiguous_dma(reason="two short vectors, once"):
                for n, vec in enumerate((ln1_g, ln1_b)):
                    for u in range(PC // C):
                        act.dma_start(pg[:, n, :, u],
                                      vec.rearrange("(u k c) -> u k c", u=PC // C, c=C)[u])\
                            .then_inc(ld_patch, 16)
            for dst, vec in ((b_patch_bc, b_patch), (ln2_g_bc, ln2_g), (ln2_b_bc, ln2_b)):
                act.dma_start(dst, vec.partition_broadcast(R)).then_inc(ld_z, 16)
            pos_v = pos_emb[0, 1:1 + G * G, :].rearrange("(a h w) e -> a h (w e)", a=1, w=G)
            act.dma_start(pos_bc.rearrange("r w e -> r (w e)"), pos_v.to_broadcast([B, G, G * E]))\
               .then_inc(ld_z, 16)
            act.dma_start(w_nat[:, 0:3 * EC, :], w_attn.rearrange("(m p) e -> p m e", p=128)).then_inc(ld_nat, 16)
            act.dma_start(w_nat[:, 3 * EC:, :], w_proj.rearrange("(m p) e -> p m e", p=128)).then_inc(ld_nat, 16)
            act.dma_start(cls_pos[:, 0, :], cls_token[0]).then_inc(ld_cls, 16)
            act.dma_start(cls_pos[:, 1, :], pos_emb[0, 0:1, :]).then_inc(ld_cls, 16)
            act.dma_start(gate_sb[:, :, :], gate_w.rearrange("(k p) x -> p k x", p=128)).then_inc(ld_const, 16)
            act.dma_start(b1_nat[:, :], b1.rearrange("x (c p) -> (x c) p", p=128)).then_inc(ld_const, 16)

            act.wait_ge(ld_patch, PATCH_LOADS)

            def patch_evict(w, par):
                act.wait_ge(px_T, w + 1)
                if not early(w, 2):
                    act.wait_ge(pz_ps, w - 1)
                for c in range(PC):
                    src = bank[2 * par + c // 3][:, (c % 3) * R:(c % 3 + 1) * R]
                    ins = act.activation(pxT[:, par, c, :], src, ACT.Identity,
                                         bias=pg[:, 1, c // 2, c % 2:c % 2 + 1],
                                         scale=pg[:, 0, c // 2, c % 2:c % 2 + 1])
                ins.then_inc(px_Tcopied, 1)

            loop_by(2, act, G, patch_evict)

            for n in range(3 * EC + EC):
                act.wait_ge(wT_ps, n + 1)
                dst = w_attnT[:, :, n * 128:(n + 1) * 128] if n < 3 * EC else \
                    w_projT[:, :, (n - 3 * EC) * 128:(n - 3 * EC + 1) * 128]
                act.activation(dst, bank[6][:, 0:EC * 128].rearrange("p (k n) -> p k n", k=EC),
                               ACT.Copy).then_inc(wT_copied, 1)
            act.wait_ge(wT_ps, 4 * EC + 1)
            act.activation(b1T[:, :], bank[6][:, 0:X * FC], ACT.Copy).then_inc(wT_copied, 1)
            act.wait_ge(v_ones, 1)

            def copy_xnT(n, par):
                act.wait_ge(xnT_ps, n + 1)
                if not early(n, 2):
                    act.wait_ge(v_ps, n - 1)
                act.activation(xnT[:, par, :, :], bank[7][:, 0:EC * T].rearrange("p (k t) -> p k t", k=EC),
                               ACT.Copy).then_inc(xnT_copied, 1)

            copy_xnT(0, 0)

            def attention(s, par):
                n, f, e, b, r = entry(s + 1), entry(s), entry(s - 1), entry(s - 2), entry(s - 3)
                A, BB = bank[0], bank[1]

                def copy_pT(g):
                    act.wait_ge(pT_ps, NG * b + g + 1)
                    if g == 0 and not early(b, 1):
                        act.wait_ge(pv_ps, b)
                    act.activation(probsT[:, HG * g:HG * (g + 1), :],
                                   bank[6 + g % 2][0:T, 0:HG * T].rearrange("p (h t) -> p h t", h=HG),
                                   ACT.Copy).then_inc(pT_copied, 1)

                def exponentiate(g):
                    act.wait_ge(shifted, NG * e + g + 1)
                    p = probs[:, 1 - par, HG * g:HG * (g + 1), :]
                    act.activation(p, p, ACT.Exp, scale=float(DK) ** -0.5).then_inc(exp_done, 1)

                if b is not None:
                    copy_pT(0)
                    copy_pT(1)
                if f is not None:
                    act.wait_ge(qk_ps, f + 1)
                    if not early(f, 1):
                        act.wait_ge(scores_ps, NG * f)
                    act.activation(qT[:, :, :], A[:, 0:EC * T].rearrange("p (k t) -> p k t", k=EC),
                                   ACT.Copy).then_inc(q_copied, 1)
                if b is not None:
                    copy_pT(2)
                    copy_pT(3)
                if e is not None:
                    exponentiate(0)
                    exponentiate(1)
                if n is not None:
                    copy_xnT(n, 1 - par)
                if r is not None:
                    act.wait_ge(x2T_ps, r + 1)
                    if not early(r, 1):
                        act.wait_ge(logit_ps, r)
                    act.activation(x2T[:, :, :], A[:, 0:EC * T].rearrange("p (k t) -> p k t", k=EC),
                                   ACT.Copy).then_inc(x2T_copied, 1)
                if f is not None:
                    act.wait_ge(v_ps, f + 1)
                    if not early(f, 2):
                        act.wait_ge(pv_ps, f - 1)
                    act.activation(v_aug[:, par, :, 0:DK],
                                   BB[0:T, 0:E].rearrange("p (h d) -> p h d", h=H), ACT.Copy)\
                       .then_inc(v_copied, 1)
                if e is not None:
                    exponentiate(2)
                if b is not None:
                    act.wait_ge(oT_ps, b + 1)
                    if not early(b, 1):
                        act.wait_ge(proj_ps, b)
                    act.activation(oT[:, :, :], BB[:, 0:EC * T].rearrange("p (k t) -> p k t", k=EC),
                                   ACT.Copy).then_inc(oT_copied, 1)
                if e is not None:
                    exponentiate(3)

            attention_steps(act, attention)

            act.wait_ge(l_shifted, 1)
            act.activation(lexp[:, :, :], lexp[:, :, :], ACT.Exp).then_inc(l_exp, 1)

            act.wait_ge(blk_ex_done, 1)

            def expert(k, par):
                e = act.value_load(blk_ex[0:1, bass.ds(k, 1)], min_val=0, max_val=X - 1)
                for c in range(FC):
                    if c % 4 == 0:
                        act.wait_ge(hidT_ps, 2 * k + c // 4 + 1)
                        if not early(k, 2):
                            act.wait_ge(y_ps, k - 1)
                    ins = act.activation(actT[:, par, c, :], bank[4 + c // 4][:, c % 4 * 128:(c % 4 + 1) * 128],
                                         ACT.Gelu, bias=b1T[:, bass.ds(e * FC + c, 1)])
                    if c % 4 == 3:
                        ins.then_inc(gelu_done, 1)

            loop_by(2, act, NBLK, expert)

        @block.tensor
        def _(pe):
            pe.wait_ge(pool_const, 7)

            def patch_T(w, par):
                pe.wait_ge(px_norm, w + 1)
                if not early(w, 2):
                    pe.wait_ge(px_Tcopied, w - 1)
                for c in range(PC):
                    ins = pe.transpose(bank[2 * par + c // 3][:, (c % 3) * R:(c % 3 + 1) * R],
                                       pxn[:, par, c * 128:(c + 1) * 128], ident[0:R, 0:R])
                ins.then_inc(px_T, 1)

            def patch_mm(w, par):
                pe.wait_ge(px_Tcopied, w + 1)
                if not early(w, 2):
                    pe.wait_ge(pz_biased, w - 1)
                for c in range(PC):
                    ins = pe.matmul(bank[4 + par][0:R, 0:E], pxT[:, par, c, :], w_patch_sb[:, c, :],
                                    start=(c == 0), stop=(c == PC - 1))
                ins.then_inc(pz_ps, 1)

            patch_T(0, 0)
            pe.wait_ge(ld_patch, PATCH_LOADS)
            patch_T(1, 1)
            patch_mm(0, 0)
            with pe.Fori(1, G // 2) as i:
                patch_T(2 * i, 0)
                patch_mm(2 * i - 1, 1)
                patch_T(2 * i + 1, 1)
                patch_mm(2 * i, 0)
            patch_mm(G - 1, 1)

            for n in range(4 * EC):
                if n == 0:
                    pe.wait_ge(ld_nat, 32)
                if n >= 1:
                    pe.wait_ge(wT_copied, n)
                for k in range(EC):
                    ins = pe.transpose(bank[6][:, k * 128:(k + 1) * 128],
                                       w_nat[:, n, k * 128:(k + 1) * 128], ident[:, :])
                ins.then_inc(wT_ps, 1)
            pe.wait_ge(wT_copied, 4 * EC)
            pe.wait_ge(ld_const, 32)
            pe.transpose(bank[6][:, 0:X * FC], b1_nat[:, :], ident[0:X * FC, 0:X * FC]).then_inc(wT_ps, 1)
            pe.wait_ge(wT_copied, 4 * EC + 1)

            def norm_T(n, par):
                pe.wait_ge(xn_ready, n + 1)
                for k in range(EC):
                    ins = pe.transpose(bank[7][:, k * T:(k + 1) * T], xn[:, par, k * 128:(k + 1) * 128],
                                       ident[0:T, 0:T])
                ins.then_inc(xnT_ps, 1)

            norm_T(0, 0)
            pe.wait_ge(px_Tcopied, G)
            pe.wait_ge(pz_biased, G)

            def attention(s, par):
                n, f, b, r = entry(s + 1), entry(s), entry(s - 2), entry(s - 3)
                A, BB = bank[0], bank[1]

                def probs_T(g):
                    pe.wait_ge(exp_done, NG * b + g + 1)
                    if g >= 2:
                        pe.wait_ge(pT_copied, NG * b + g - 1)
                    elif g == 1 and f is not None:
                        pe.wait_ge(xnT_copied, f + 1)
                    elif g == 0 and not early(b, 1):
                        pe.wait_ge(o_done, b)
                    for j in range(HG):
                        ins = pe.transpose(bank[6 + g % 2][0:T, j * T:(j + 1) * T],
                                           probs[:, par, HG * g + j, :], ident[0:T, 0:T])
                    ins.then_inc(pT_ps, 1)

                def weighted_v(g):
                    for h in range(HG * g, HG * (g + 1)):
                        ins = pe.matmul(bank[6][0:T, h * (DK + 1):(h + 1) * (DK + 1)], probsT[:, h, :],
                                        v_aug[:, par, h, :], start=True, stop=True)
                    if g == NG - 1:
                        ins.then_inc(pv_ps, 1)

                def scores(g):
                    c, h = HG * g // (H // EC), HG * g % (H // EC)
                    pe.matmul(bank[2 + g][0:T, 0:HG * T], qT[:, c, :],
                              k_heads[:, c, h:h + HG, :].rearrange("p h t -> p (h t)"),
                              start=False, stop=True).then_inc(scores_ps, 1)

                if b is not None:
                    probs_T(0)
                    probs_T(1)
                if f is not None:
                    pe.wait_ge(xnT_copied, f + 1)
                    if not early(f, 4):
                        pe.wait_ge(x2T_copied, f - 3)
                    elif f >= 1:
                        pe.wait_ge(k_copied, f)
                    for m in range(2 * EC):
                        for k in range(EC):
                            ins = pe.matmul(A[:, m * T:(m + 1) * T], w_attnT[:, k, m * 128:(m + 1) * 128],
                                            xnT[:, par, k, :], start=(k == 0), stop=(k == EC - 1))
                    ins.then_inc(qk_ps, 1)
                if b is not None:
                    probs_T(2)
                    probs_T(3)
                if f is not None:
                    if not early(f, 3):
                        pe.wait_ge(resid_done, f - 2)
                    elif f >= 1:
                        pe.wait_ge(v_copied, f)
                    if not early(f, 4):
                        pe.wait_ge(logit_kept, f - 3)
                    for k in range(EC):
                        ins = pe.matmul(BB[0:T, 0:E], xnT[:, par, k, :], w_attnT[:, k, 2 * E:3 * E],
                                        start=(k == 0), stop=(k == EC - 1))
                    ins.then_inc(v_ps, 1)
                    for g in range(NG):
                        if not early(f, 1):
                            pe.wait_ge(shifted, NG * (f - 1) + g + 1)
                        pe.matmul(bank[2 + g][0:T, 0:HG * T], ident_bf[:, :],
                                  mask_bf[:, :, :].rearrange("p h t -> p (h t)"), start=True, stop=False)
                if b is not None:
                    pe.wait_ge(pT_copied, NG * (b + 1))
                    pe.wait_ge(v_copied, b + 1)
                    weighted_v(0)
                    weighted_v(1)
                if n is not None:
                    norm_T(n, 1 - par)
                if b is not None:
                    weighted_v(2)
                    weighted_v(3)
                if f is not None:
                    pe.wait_ge(q_copied, f + 1)
                    pe.wait_ge(k_copied, f + 1)
                if r is not None:
                    pe.wait_ge(x2n_ready, r + 1)
                    if f is None:
                        pe.wait_ge(x2T_copied, r)
                    for k in range(EC):
                        ins = pe.transpose(A[:, k * T:(k + 1) * T], x2[:, 1 - par, k * 128:(k + 1) * 128],
                                           ident[0:T, 0:T])
                    ins.then_inc(x2T_ps, 1)
                if f is not None:
                    for g in range(NG - 1):
                        scores(g)
                if b is not None:
                    pe.wait_ge(o_done, b + 1)
                    if f is not None:
                        pe.wait_ge(v_copied, f + 1)
                    else:
                        pe.wait_ge(resid_done, b)
                        pe.wait_ge(logit_kept, b - 1)
                    for k in range(EC):
                        ins = pe.transpose(BB[:, k * T:(k + 1) * T], o_sb[:, k * 128:(k + 1) * 128],
                                           ident[0:T, 0:T])
                    ins.then_inc(oT_ps, 1)
                if f is not None:
                    scores(NG - 1)
                if b is not None:
                    pe.wait_ge(oT_copied, b + 1)
                if r is not None:
                    pe.wait_ge(x2T_copied, r + 1)
                    if b is None:
                        pe.wait_ge(logit_kept, r)
                        pe.wait_ge(resid_done, B)
                    for k in range(EC):
                        ins = pe.matmul(BB[0:T, E:E + X], x2T[:, k, :], gate_sb[:, k, :],
                                        start=(k == 0), stop=(k == EC - 1))
                    ins.then_inc(logit_ps, 1)
                if b is not None:
                    for k in range(EC):
                        ins = pe.matmul(BB[0:T, 0:E], oT[:, k, :], w_projT[:, k, :],
                                        start=(k == 0), stop=(k == EC - 1))
                    ins.then_inc(proj_ps, 1)

            attention_steps(pe, attention)

            pe.wait_ge(chosen_done, 1)
            picks = chosen_bf[:, :, :].rearrange("p b x -> p (b x)")
            pe.matmul(bank[0][0:T, 0:B * X], before[:, :], picks, start=True, stop=False)
            for d in range(1, B):
                ins = pe.matmul(bank[0][0:T, d * X:B * X], ones_bf[:, :], picks[:, 0:(B - d) * X],
                                start=False, stop=(d == B - 1))
            pe.matmul(bank[1][0:T, 0:B * X], ones_bf[:, :], picks, start=True, stop=True).then_inc(rank_ps, 1)

            pe.wait_ge(blk_ex_done, 1)
            for e in range(X):
                pe.wait_ge(ld_w[e], 32)

            def block_T(k, slot):
                pe.wait_ge(ld_blk[slot], 16 // RING * (k - slot) + 16)
                if not early(k, 1):
                    pe.wait_ge(blkT_copied, k)
                for c in range(EC):
                    ins = pe.transpose(bank[6][:, c * 128:(c + 1) * 128],
                                       blk_in[:, slot, c * 128:(c + 1) * 128], ident[:, :])
                ins.then_inc(blkT_ps, 1)

            def hidden(k, par):
                e = pe.value_load(blk_ex[0:1, bass.ds(k, 1)], min_val=0, max_val=X - 1)
                pe.wait_ge(blkT_copied, k + 1)
                if not early(k, 2):
                    pe.wait_ge(hid_copied, 2 * (k - 1))
                for n in range(F // 512):
                    for c in range(EC):
                        ins = pe.matmul(bank[2 * par + n][:, :], blkT[:, par, c, :],
                                        w1_sb[:, bass.ds(e, 1), c, n * 512:(n + 1) * 512],
                                        start=(c == 0), stop=(c == EC - 1))
                    ins.then_inc(hid_ps, 1)

            def hidden_T(k, par):
                for n in range(2):
                    pe.wait_ge(hid_copied, 2 * k + n + 1)
                    if not early(k, 1):
                        pe.wait_ge(gelu_done, 2 * k + n - 1)
                    for c in range(FC // 2):
                        ins = pe.transpose(bank[4 + n][:, c * 128:(c + 1) * 128],
                                           hid[:, par, (4 * n + c) * 128:(4 * n + c + 1) * 128], ident[:, :])
                    ins.then_inc(hidT_ps, 1)

            def down(k, par):
                e = pe.value_load(blk_ex[0:1, bass.ds(k, 1)], min_val=0, max_val=X - 1)
                if not early(k, 1):
                    pe.wait_ge(y_biased, k)
                for c in range(FC):
                    if c % 4 == 0:
                        pe.wait_ge(gelu_done, 2 * k + c // 4 + 1)
                    ins = pe.matmul(bank[7][:, 0:E], actT[:, par, c, :], w2_sb[:, bass.ds(e, 1), c, :],
                                    start=(c == 0), stop=(c == FC - 1))
                ins.then_inc(y_ps, 1)

            def turn(k, slot, more=True):
                par = slot % 2
                hidden_T(k, par)
                hidden(k + 1, 1 - par)
                if more:
                    block_T(k + 2, (slot + 2) % RING)
                down(k, par)

            block_T(0, 0)
            hidden(0, 0)
            block_T(1, 1)
            loop_by(RING, pe, NBLK - 2, turn)
            turn(NBLK - 2, 0, more=False)
            hidden_T(NBLK - 1, 1)
            down(NBLK - 1, 1)

        @block.vector
        def _(dve):
            patches = px.rearrange("r c (p w q) -> r c w p q", p=PS, w=G)

            def patch_stats(w):
                for c in range(C):
                    if w == 0:
                        dve.wait_ge(ld_x[c], 16)
                    ins = dve.bn_stats(px_six[:, w, c, :], patches[:, c, w])
                ins.then_inc(p_chain, 1)
                dve.wait_ge(p_chain, w + 1)
                dve.bn_aggr(pmv[:, w, :], px_six[:, w, :, :]).then_inc(px_stats, 1)

            def patch_norm(w):
                dve.wait_ge(px_rstd, w + 1)
                if w >= 2:
                    dve.wait_ge(px_T, w - 1)
                dve.tensor_scalar(pxn[:, w % 2, :].rearrange("r (c p q) -> r c p q", c=C, p=PS),
                                  patches[:, :, w], prs[:, w, 0:1], prs[:, w, 1:2],
                                  ALU.mult, ALU.subtract).then_inc(px_norm, 1)

            def proj_stats(w):
                dve.wait_ge(pz_ps, w + 1)
                if w >= 2:
                    dve.wait_ge(st_patch[w % 2], 16 * (w // 2))
                dve.tensor_tensor(pz[:, w % 2, :], bank[4 + w % 2][0:R, 0:E], b_patch_bc, ALU.add)\
                   .then_inc(pz_biased, 1)
                dve.wait_ge(pz_biased, w + 1)
                dve.bn_stats(pz_six[:, w, :], pz[:, w % 2, :]).then_inc(pz_chain, 1)
                dve.wait_ge(pz_chain, 3 * w + 1)
                dve.bn_aggr(zmv[:, w, :], pz_six[:, w, :]).then_inc(pz_stats, 1)

            def proj_norm(w):
                z = pz[:, w % 2, :]
                dve.wait_ge(pz_rstd, w + 1)
                dve.tensor_scalar(z, z, zrs[:, w, 0:1], zrs[:, w, 1:2], ALU.mult, ALU.subtract).then_inc(pz_chain, 1)
                dve.wait_ge(pz_chain, 3 * w + 2)
                dve.tensor_tensor(z, z, ln2_g_bc, ALU.mult).then_inc(pz_chain, 1)
                dve.wait_ge(pz_chain, 3 * w + 3)
                dve.tensor_tensor(z, z, pos_bc[:, w, :], ALU.add).then_inc(pz_done, 1)

            patch_stats(0)
            for w in range(G + 2):
                if w + 1 < G:
                    patch_stats(w + 1)
                if w < G:
                    patch_norm(w)
                if w == 2:
                    dve.wait_ge(ld_cls, 32)
                    dve.tensor_tensor(cls_pos[:, 0, :], cls_pos[:, 0, :], cls_pos[:, 1, :], ALU.add)\
                       .then_inc(cls_done, 1)
                    dve.wait_ge(ld_z, 16 * 4)
                    dve.wait_ge(posb_done, 1)
                if w >= 2:
                    proj_stats(w - 2)
                    proj_norm(w - 2)

            dve.wait_ge(ld_txt, 32)
            dve.wait_ge(ld_tok, 16)
            for n, entries in enumerate(LN1_GROUPS):
                for b in entries:
                    ins = dve.bn_stats(six1[:, b, :], rows[:, b, RES:RES + E])
                ins.then_inc(ln1_chain, 1)
                dve.wait_ge(ln1_chain, n + 1)
                for b in entries:
                    ins = dve.bn_aggr(mv1[:, b, :], six1[:, b, :])
                ins.then_inc(ln1_stats, 1)

            dve.wait_ge(pool_const, 14)

            def attention(s, par):
                f, b, r = entry(s), entry(s - 2), entry(s - 3)
                A, BB = bank[0], bank[1]
                if f is not None:
                    dve.wait_ge(q_copied, f + 1)
                    if not early(f, 1):
                        dve.wait_ge(scores_ps, NG * f)
                    for c in range(EC):
                        k_c = A[:, (EC + c) * T:(EC + c + 1) * T]
                        ins = dve.tensor_tensor(k_heads[:, c, :, :], k_c.unsqueeze(1).to_broadcast([128, H // EC, T]),
                                                head_of[:, :].unsqueeze(2).to_broadcast([128, H // EC, T]), ALU.mult)
                    ins.then_inc(k_copied, 1)
                if b is not None:
                    ov = bank[6][0:T, 0:H * (DK + 1)].rearrange("p (h d) -> p h d", h=H)
                    dve.wait_ge(pv_ps, b + 1)
                    dve.reciprocal(rsum[:, :], ov[:, :, DK]).then_inc(rsum_done, 1)
                    dve.wait_ge(rsum_done, b + 1)
                    if not early(b, 1):
                        dve.wait_ge(oT_ps, b)
                    dve.tensor_tensor(o_sb.rearrange("p (h d) -> p h d", h=H), ov[:, :, 0:DK],
                                      rsum[:, :].unsqueeze(2).to_broadcast([T, H, DK]), ALU.mult)\
                       .then_inc(o_done, 1)
                if f is not None:
                    for g in range(NG + 1):
                        if g < NG:
                            dve.wait_ge(scores_ps, NG * f + g + 1)
                            dve.tensor_reduce(smax[:, par, HG * g:HG * (g + 1)],
                                              bank[2 + g][0:T, 0:HG * T].rearrange("p (h t) -> p h t", h=HG),
                                              AX.X, ALU.max).then_inc(max_done, 1)
                        if g >= 1:
                            heads = slice(HG * (g - 1), HG * g)
                            dve.wait_ge(max_done, NG * f + g)
                            if g == 1 and not early(f, 2):
                                dve.wait_ge(pT_ps, NG * (f - 1))
                            dve.tensor_tensor(probs[:, par, heads, :],
                                              bank[1 + g][0:T, 0:HG * T].rearrange("p (h t) -> p h t", h=HG),
                                              smax[:, par, heads].unsqueeze(2).to_broadcast([T, HG, T]),
                                              ALU.subtract).then_inc(shifted, 1)
                if b is not None:
                    res = x2[:, par, RES:RES + E]
                    dve.wait_ge(proj_ps, b + 1)
                    if not early(b, 2):
                        dve.wait_ge(x2_kept, b - 1)
                    dve.tensor_tensor(res, BB[0:T, 0:E], rows[:, b, RES:RES + E], ALU.add).then_inc(resid_done, 1)
                    dve.wait_ge(resid_done, b + 1)
                    dve.bn_stats(six2[:, par, :], res).then_inc(ln2_chain, 1)
                    dve.wait_ge(ln2_chain, b + 1)
                if r is not None:
                    dve.wait_ge(logit_ps, r + 1)
                    dve.tensor_copy(logits[:, r, :], BB[0:T, E:E + X]).then_inc(logit_kept, 1)
                if b is not None:
                    dve.bn_aggr(mv2[:, par, :], six2[:, par, :]).then_inc(ln2_stats, 1)

            attention_steps(dve, attention)

            steps = [0]

            def then(ins):
                steps[0] += 1
                ins.then_inc(r_chain, 1)
                dve.wait_ge(r_chain, steps[0])

            over_x = lambda v: v.unsqueeze(2).to_broadcast([T, B, X])
            over_b = lambda v: v.unsqueeze(1).to_broadcast([T, B, X])
            dve.wait_ge(logit_kept, B)
            then(dve.tensor_reduce(lmax[:, :], logits[:, :, :], AX.X, ALU.max))
            dve.tensor_tensor(lexp[:, :, :], logits[:, :, :], over_x(lmax[:, :]), ALU.subtract)\
               .then_inc(l_shifted, 1)
            then(dve.tensor_tensor(lkey[:, :, :], logits[:, :, :], over_x(lmax[:, :]), ALU.is_equal))
            then(dve.scalar_tensor_tensor(out=lkey[:, :, :], in0=lkey[:, :, :], scalar=float(-X),
                                          in1=over_b(expert_no[:, :]), op0=ALU.mult, op1=ALU.add))
            then(dve.tensor_reduce(lfirst[:, :], lkey[:, :, :], AX.X, ALU.min))
            then(dve.tensor_tensor(chosen[:, :, :], lkey[:, :, :], over_x(lfirst[:, :]), ALU.is_equal))
            dve.tensor_copy(chosen_bf[:, :, :], chosen[:, :, :]).then_inc(chosen_done, 1)
            dve.wait_ge(rank_ps, 1)
            then(dve.tensor_reduce(count[:, :], bank[1][0:T, 0:B * X].rearrange("p (b x) -> p x b", b=B),
                                   AX.X, ALU.add))
            then(dve.tensor_tensor(many[:, :, :], count[:, :].unsqueeze(2).to_broadcast([T, X, NFULL]),
                                   filled[:, :].unsqueeze(1).to_broadcast([T, X, NFULL]), ALU.is_gt))
            then(dve.tensor_reduce(nblk[:, :], many[:, :, :], AX.X, ALU.add))
            then(dve.tensor_tensor_scan(blk_end[:, :], ones_f[:, :], nblk[:, :], 0.0, ALU.mult, ALU.add))
            then(dve.tensor_tensor(start[:, :], blk_end[:, :], nblk[:, :], ALU.subtract))
            then(dve.tensor_scalar(start[:, :], start[:, :], float(SLOT), None, ALU.mult))
            then(dve.tensor_tensor(slot_of[:, :, :], bank[0][0:T, 0:B * X].rearrange("p (b x) -> p b x", b=B),
                                   over_b(start[:, :]), ALU.add))
            then(dve.tensor_tensor(slot_of[:, :, :], slot_of[:, :, :], chosen[:, :, :], ALU.mult))
            then(dve.tensor_reduce(pos_f[:, :], slot_of[:, :, :], AX.X, ALU.add))
            dve.tensor_copy(pos[:, :], pos_f[:, :]).then_inc(pos_done, 1)
            dve.wait_ge(l_exp, 1)
            then(dve.tensor_reduce(lsum[:, :], lexp[:, :, :], AX.X, ALU.add))
            dve.reciprocal(rows[:, :, WGT], lsum[:, :]).then_inc(weight_done, 1)
            then(dve.tensor_tensor(blk_cmp[:, :, :], blk_no[:, :].unsqueeze(2).to_broadcast([1, NBLK, X]),
                                   blk_end[0:1, :].unsqueeze(1).to_broadcast([1, NBLK, X]), ALU.is_ge))
            then(dve.tensor_reduce(blk_ex_f[:, :], blk_cmp[:, :, :], AX.X, ALU.add))
            dve.tensor_scalar(blk_ex[:, :], blk_ex_f[:, :], float(X - 1), None, ALU.min).then_inc(blk_ex_done, 1)
            dve.wait_ge(blk_ex_done, 1)
            dve.wait_ge(ld_b2, 16)

            def copy_block(k, par):
                dve.wait_ge(blkT_ps, k + 1)
                if not early(k, 2):
                    dve.wait_ge(hid_ps, 2 * (k - 1))
                dve.tensor_copy(blkT[:, par, :, :], bank[6][:, 0:E].rearrange("p (c t) -> p c t", c=EC))\
                   .then_inc(blkT_copied, 1)

            def copy_hidden(k, par):
                for n in range(2):
                    dve.wait_ge(hid_ps, 2 * k + n + 1)
                    if not early(k, 2):
                        dve.wait_ge(hidT_ps, 2 * (k - 2) + n + 1)
                    dve.tensor_copy(hid[:, par, n * 512:(n + 1) * 512], bank[2 * par + n][:, :])\
                       .then_inc(hid_copied, 1)

            def finish_block(k, slot):
                par = slot % 2
                e = dve.value_load(blk_ex[0:1, bass.ds(k, 1)], min_val=0, max_val=X - 1)
                y = blk_out[:, par, :]
                dve.wait_ge(y_ps, k + 1)
                if not early(k, 2):
                    dve.wait_ge(st_out[par], 8 * (k - par))
                dve.tensor_tensor(y, bank[7][:, 0:E], b2_bc[:, e, :], ALU.add).then_inc(y_biased, 1)
                dve.wait_ge(y_biased, k + 1)
                dve.wait_ge(ld_blk[slot], 16 // RING * (k - slot) + 16)
                dve.scalar_tensor_tensor(out=y, in0=y, scalar=blk_in[:, slot, WGT:WGT + 1],
                                         in1=blk_in[:, slot, RES:RES + E], op0=ALU.mult, op1=ALU.add)\
                   .then_inc(blk_done, 1)

            def turn(k, slot, more=True):
                copy_hidden(k + 1, 1 - slot % 2)
                if more:
                    copy_block(k + 2, slot % 2)
                finish_block(k, slot)

            copy_block(0, 0)
            copy_hidden(0, 0)
            copy_block(1, 1)
            loop_by(RING, dve, NBLK - 2, turn)
            turn(NBLK - 2, (NBLK - 2) % RING, more=False)
            finish_block(NBLK - 1, (NBLK - 1) % RING)


_INS = ["x", "txt", "L0_tok_ln1_g", "L0_tok_ln1_b", "L0_tok_W_proj", "L0_tok_b_proj", "L0_tok_ln2_g",
        "L0_tok_ln2_b", "L0_tok_cls_token", "L0_tok_pos_emb", "L0_attn_w_attn", "L0_attn_w_proj",
        "L0_ffn_gate_w", "L0_ffn_w1", "L0_ffn_b1", "L0_ffn_w2", "L0_ffn_b2"]


def kernel(**inputs):
    import numpy as _np
    import concourse.bacc as _bacc
    from concourse import mybir as _mybir
    from concourse.bass_utils import run_bass_kernel_spmd as _run

    nc = _bacc.Bacc("TRN2", target_bir_lowering=False, num_devices=1)
    arrays, args = {}, []
    for name in _INS:
        a = _np.ascontiguousarray(inputs[name])
        arrays[f"in_{name}_dram"] = a
        args.append(nc.dram_tensor(f"in_{name}_dram", a.shape, _mybir.dt.from_np(a.dtype),
                                   kind="ExternalInput").ap())
    images, _, _, _ = inputs["x"].shape
    tokens = inputs["L0_tok_pos_emb"].shape[1] + inputs["txt"].shape[1]
    shape = (images, tokens, inputs["txt"].shape[2])
    args.append(nc.dram_tensor("out_0_dram", shape, _mybir.dt.float32, kind="ExternalOutput").ap())
    fusion_program(nc, *args)
    r = _run(nc, [arrays], core_ids=[0])
    return r.results[0]["out_0_dram"]
```

```python
from contextlib import ExitStack

import concourse.bass as bass
from concourse import mybir

ALU = mybir.AluOpType
ACT = mybir.ActivationFunctionType
AX = mybir.AxisListType
F32 = mybir.dt.float32
BF16 = mybir.dt.bfloat16
F32R = mybir.dt.float32r
I32 = mybir.dt.int32
U32 = mybir.dt.uint32
LN_EPS = 1e-5
MASKED = -1e30


def loop_by(unroll, eng, count, step):
    rest = count % unroll
    for n in range(unroll + rest):
        step(n, n % unroll)
    with eng.Fori(1, count // unroll) as i:
        for n in range(rest, rest + unroll):
            step(unroll * i + n, n % unroll)


def fusion_program(nc, x, txt, ln1_g, ln1_b, w_patch, b_patch, ln2_g, ln2_b, cls_token, pos_emb,
                   w_attn, w_proj, gate_w, w1, b1, w2, b2, out):
    B, C, HH, _ = x.shape
    S, E = txt.shape[1:]
    PS = 16
    G = HH // PS
    T = 1 + G * G + S
    R = B * G
    PD = C * PS * PS
    PC = PD // 128
    EC = E // 128
    H, DK = 16, E // 16
    X, _, F = w1.shape
    FC = F // 128
    SLOT = 128
    NBLK = (B * T + X * (SLOT - 1)) // SLOT
    NBLK += NBLK % 2
    NFULL = -(-B * T // SLOT)
    RES = E
    NOBODY = 1 << 20
    RING = 4
    PIECES = 3
    HG = 4
    NG = H // HG

    token_rows = nc.dram_tensor("token_rows", [B * T, 2 * E], F32)
    patch_rows = nc.dram_tensor("patch_rows", [G, R, E], F32)
    out_rows = out.rearrange("b t d -> (b t) d")

    with ExitStack() as ctx:
        def sb(name, shape, dt=F32):
            return ctx.enter_context(nc.sbuf_tensor(name, shape, dt))

        def sem(name):
            return ctx.enter_context(nc.semaphore(name))

        experts = sb("experts", [128, X, EC * F + FC * E])
        w1_sb = experts[:, :, 0:EC * F].rearrange("p e (k f) -> p e k f", k=EC)
        w2_sb = experts[:, :, EC * F:].rearrange("p e (c d) -> p e c d", c=FC)
        rows_room = sb("rows_room", [128, max(B * E, 2 * EC * F)])
        rows = rows_room[0:T, 0:B * E].rearrange("p (b n) -> p b n", b=B)
        w1_now = rows_room[:, 0:2 * EC * F].rearrange("p (s k f) -> p s k f", s=2, k=EC)
        w2_last = rows_room[:, 0:FC * E].rearrange("p (c d) -> p c d", c=FC)

        def carver(room):
            taken = [0]

            def carve(width):
                taken[0] += width
                assert taken[0] <= room.shape[1]
                return room[:, taken[0] - width:taken[0]]
            return carve

        carve = carver(experts[:, X - 4:X - 1, :].rearrange("p e n -> p (e n)"))
        px = carve(C * PS * HH).rearrange("p (c n) -> p c n", c=C)[0:R]
        pxn = carve(2 * PD).rearrange("p (s n) -> p s n", s=2)[0:R]
        w_patch_sb = carve(PC * E).rearrange("p (c e) -> p c e", c=PC)
        w_nat = carve(4 * EC * E).rearrange("p (n e) -> p n e", n=4 * EC)
        b1_nat = carve(128)[0:X * FC]
        probs = experts[:, X - 1, 0:2 * H * T].rearrange("p (s h t) -> p s h t", s=2, h=H)[0:T]
        carve = carver(experts[:, X - 2, :])
        probsT = carve(H * T).rearrange("p (h t) -> p h t", h=H)[0:T]

        WORK = 5120
        work = sb("work", [128, WORK])
        carve = carver(work[:, :])
        pxT = carve(2 * PC * R).rearrange("p (s c r) -> p s c r", s=2, c=PC)
        pz = carve(2 * E).rearrange("p (s n) -> p s n", s=2)[0:R]
        b_patch_sb = carve(E)[0:1]
        ones_row = carve(R)[0:1]
        ln2_g_bc = carve(E)[0:R]
        ln2_b_bc = carve(E)[0:R]
        pos_bc = carve(G * E).rearrange("p (w n) -> p w n", w=G)[0:R]
        cls_pos = carve(2 * E).rearrange("p (s n) -> p s n", s=2)[0:1]
        carve = carver(work[:, :])
        xn = carve(2 * E).rearrange("p (s n) -> p s n", s=2)[0:T]
        xnT = carve(2 * EC * T).rearrange("p (s k t) -> p s k t", s=2, k=EC)
        v_aug = carve(2 * H * (DK + 1)).rearrange("p (s h d) -> p s h d", s=2, h=H)[0:T]
        o_sb = carve(E)[0:T]
        oT = carve(EC * T).rearrange("p (k t) -> p k t", k=EC)
        x2 = carve(4 * E).rearrange("p (s n) -> p s n", s=2)[0:T]
        x2T = carve(EC * T).rearrange("p (k t) -> p k t", k=EC)
        carve = carver(work[:, :])
        in_slot = carve(B * SLOT // 2).bitcast(BF16).rearrange("p (b s) -> p b s", b=B)[0:T]
        tagged = carve(B * (2 + PIECES) * NBLK // 2).bitcast(BF16)\
            .rearrange("p (b f k) -> p b f k", b=B, f=2 + PIECES)[0:T]
        carve = carver(work[:, :])
        actT = carve(2 * F).rearrange("p (s c t) -> p s c t", s=2, c=FC)
        blk_out = carve(2 * E).rearrange("p (s n) -> p s n", s=2)
        blkT = carve(2 * E).rearrange("p (s c t) -> p s c t", s=2, c=EC)
        blk_in = carve(RING * 2 * E).rearrange("p (s n) -> p s n", s=RING)
        act_up = sb("act_up", [128, FC, SLOT], F32R)
        act_low = sb("act_low", [128, FC, SLOT], F32R)
        w2_up = sb("w2_up", [128, FC, E], F32R)
        w2_low = sb("w2_low", [128, FC, E], F32R)
        qk_up, qk_low = [v[:, :, :].rearrange("p c t -> p (c t)")[:, 0:2 * EC * T]
                         .rearrange("p (n k t) -> p n k t", n=2, k=EC) for v in (act_up, act_low)]
        heads_up, heads_low = [v[:, :, :].rearrange("p c e -> p (c e)")[:, 0:H * T]
                               .rearrange("p (k h t) -> p k h t", k=EC, h=H // EC) for v in (w2_up, w2_low)]

        attn_w = sb("attn_w", [128, EC * 3 * E + EC * E])
        w_attnT = attn_w[:, 0:EC * 3 * E].rearrange("p (k n) -> p k n", k=EC)
        w_projT = attn_w[:, EC * 3 * E:].rearrange("p (k n) -> p k n", k=EC)
        b2_bc = attn_w[:, 0:X * E].rearrange("p (x e) -> p x e", x=X)

        gate_sb = sb("gate_sb", [128, EC, X])
        b1T = sb("b1T", [128, X * FC])
        ident = sb("ident", [128, 128])
        ident_bf = sb("ident_bf", [T, T], BF16)
        mask_bf = sb("mask_bf", [T, HG, T], BF16)
        before = sb("before", [T, T], BF16)
        ones_bf = sb("ones_bf", [T, T], BF16)
        head_of = sb("head_of", [128, H // EC])
        minus_half = sb("minus_half", [128, B])
        eps = sb("eps", [128, B])
        pg = sb("pg", [128, 2, C, PC // C])
        px_six = sb("px_six", [R, G, C, 6])
        pz_six = sb("pz_six", [R, G, 6])
        pmv = sb("pmv", [R, G, 2])
        prs = sb("prs", [R, G, 2])
        zmv = sb("zmv", [R, G, 2])
        zrs = sb("zrs", [R, G, 2])
        six1 = sb("six1", [T, B, 6])
        six2 = sb("six2", [T, 2, 6])
        mv1 = sb("mv1", [T, B, 2])
        rs1 = sb("rs1", [T, B, 2])
        mv2 = sb("mv2", [T, 2, 2])
        rs2 = sb("rs2", [T, 2, 2])
        smax = sb("smax", [T, 2, H])
        rsum = sb("rsum", [T, H])
        logits = sb("logits", [T, B, X])
        lmax = sb("lmax", [T, B])
        lexp = sb("lexp", [T, B, X])
        lsum = sb("lsum", [T, B])
        lkey = sb("lkey", [T, B, X])
        lfirst = sb("lfirst", [T, B])
        chosen = sb("chosen", [T, B, X])
        chosen_bf = sb("chosen_bf", [T, B, X], BF16)
        expert_no = sb("expert_no", [T, X])
        filled = sb("filled", [T, NFULL])
        many = sb("many", [T, X, NFULL])
        count = sb("count", [T, X])
        nblk = sb("nblk", [T, X])
        blk_end = sb("blk_end", [T, X])
        start = sb("start", [T, X])
        slot_of = sb("slot_of", [T, B, X])
        pos_f = sb("pos_f", [T, B])
        pos = sb("pos", [T, B], I32)
        slot_i = sb("slot_i", [T, 2, B], I32)
        slot_f = sb("slot_f", [T, 2, B], BF16)
        slot_no = sb("slot_no", [T, SLOT], BF16)
        blk_no = sb("blk_no", [T, NBLK], BF16)
        in_blk = sb("in_blk", [T, B, NBLK], BF16)
        tags = sb("tags", [T, B, 2 + PIECES], BF16)
        weight = sb("weight", [T, B])
        token_of = sb("token_of", [SLOT, NBLK])
        vacant = sb("vacant", [SLOT, NBLK])
        from_row = sb("from_row", [SLOT, NBLK], I32)
        to_row = sb("to_row", [SLOT, NBLK], I32)
        slot_weight = sb("slot_weight", [SLOT, NBLK])
        blk_cmp = sb("blk_cmp", [1, NBLK, X])
        blk_ex_f = sb("blk_ex_f", [1, NBLK])
        blk_ex = sb("blk_ex", [1, NBLK], I32)
        ones_f = sb("ones_f", [T, X])
        unused = sb("unused", [1, 1])

        bank = [ctx.enter_context(nc.psum_tensor(f"bank{i}", [128, 512], F32)) for i in range(8)]

        ld_x = [sem(f"ld_x{c}") for c in range(C)]
        ld_patch = sem("ld_patch")
        ld_z = sem("ld_z")
        ld_const = sem("ld_const")
        ld_nat = sem("ld_nat")
        ld_cls = sem("ld_cls")
        ld_txt = sem("ld_txt")
        ld_tok = sem("ld_tok")
        ld_w = [sem(f"ld_w{e}") for e in range(X)]
        st_patch = [sem("st_patch0"), sem("st_patch1")]
        st_x2 = [sem("st_x2_0"), sem("st_x2_1")]
        ld_blk = [sem(f"ld_blk{s}") for s in range(RING)]
        ld_b2 = sem("ld_b2")
        st_out = [sem("st_out0"), sem("st_out1")]
        pool_const = sem("pool_const")
        pool_chain = sem("pool_chain")
        cls_done = sem("cls_done")
        v_ones = sem("v_ones")
        px_stats = sem("px_stats")
        px_rstd = sem("px_rstd")
        px_norm = sem("px_norm")
        px_T = sem("px_T")
        px_Tcopied = sem("px_Tcopied")
        pz_ps = sem("pz_ps")
        pz_stats = sem("pz_stats")
        pz_rstd = sem("pz_rstd")
        pz_normed = sem("pz_normed")
        pz_scaled = sem("pz_scaled")
        pz_done = sem("pz_done")
        px_pool = sem("px_pool")
        pz_pool = sem("pz_pool")
        p_chain = sem("p_chain")
        pz_chain = sem("pz_chain")
        posb_done = sem("posb_done")
        wT_ps = sem("wT_ps")
        wT_copied = sem("wT_copied")
        ln1_chain = sem("ln1_chain")
        ln1_stats = sem("ln1_stats")
        ln1_pool = sem("ln1_pool")
        xn_scaled = sem("xn_scaled")
        xn_ready = sem("xn_ready")
        xnT_ps = sem("xnT_ps")
        xnT_copied = sem("xnT_copied")
        qk_ps = sem("qk_ps")
        qk_upper = sem("qk_upper")
        qk_split = sem("qk_split")
        heads_upper = sem("heads_upper")
        heads_lower = sem("heads_lower")
        v_ps = sem("v_ps")
        v_copied = sem("v_copied")
        scores_ps = sem("scores_ps")
        max_done = sem("max_done")
        shifted = sem("shifted")
        exp_done = sem("exp_done")
        pT_ps = sem("pT_ps")
        pT_copied = sem("pT_copied")
        pv_ps = sem("pv_ps")
        rsum_done = sem("rsum_done")
        o_done = sem("o_done")
        oT_ps = sem("oT_ps")
        oT_copied = sem("oT_copied")
        proj_ps = sem("proj_ps")
        resid_done = sem("resid_done")
        ln2_chain = sem("ln2_chain")
        ln2_stats = sem("ln2_stats")
        ln2_pool = sem("ln2_pool")
        ln2_rstd = sem("ln2_rstd")
        x2n_ready = sem("x2n_ready")
        x2T_ps = sem("x2T_ps")
        x2T_copied = sem("x2T_copied")
        logit_ps = sem("logit_ps")
        logit_kept = sem("logit_kept")
        r_chain = sem("r_chain")
        l_shifted = sem("l_shifted")
        l_exp = sem("l_exp")
        chosen_done = sem("chosen_done")
        early_ranks_ps = sem("early_ranks_ps")
        rank_ps = sem("rank_ps")
        in_slot_done = sem("in_slot_done")
        in_blk_done = sem("in_blk_done")
        tokens_tagged = sem("tokens_tagged")
        weights_tagged = sem("weights_tagged")
        tokens_ps = sem("tokens_ps")
        weights_ps = sem("weights_ps")
        from_row_done = sem("from_row_done")
        to_row_done = sem("to_row_done")
        blk_ex_done = sem("blk_ex_done")
        blkT_ps = sem("blkT_ps")
        blkT_copied = sem("blkT_copied")
        hid_ps = sem("hid_ps")
        w1_copied = sem("w1_copied")
        w2_copied = sem("w2_copied")
        w2_upper = sem("w2_upper")
        w2_split = sem("w2_split")
        act_upper = sem("act_upper")
        act_split = sem("act_split")
        gelu_done = sem("gelu_done")
        y_ps = sem("y_ps")
        y_biased = sem("y_biased")
        blk_done = sem("blk_done")

        LN1_EARLY, PEELED = 2, 4
        later = -(-(B - 2 * LN1_EARLY) // PEELED)
        LN1_GROUPS = [range(2 * n, 2 * n + 2) for n in range(LN1_EARLY)] + \
            [range(n, min(n + later, B)) for n in range(2 * LN1_EARLY, B, later)]

        PATCH_LOADS = 16 * (3 * (PC // C) + 1)

        def attention_steps(eng, step):
            for s in range(PEELED):
                step(s, s % 2)
            with eng.Fori(2, B // 2 - 1) as i:
                step(2 * i, 0)
                step(2 * i + 1, 1)
            for s in range(B - 2, B + 3):
                step(s, s % 2)

        def side_by_side(eng, heads, qk, c):
            shape = [128, H // EC, T]
            return eng.tensor_tensor(heads[:, c, :, :], qk[:, 1, c, :].bitcast(F32).unsqueeze(1).to_broadcast(shape),
                                     head_of[:, :].unsqueeze(2).to_broadcast(shape), ALU.mult)

        def tag(eng, first, last):
            shape = [T, B, last - first, NBLK]
            return eng.tensor_tensor(tagged[:, :, first:last, :], in_blk[:, :, :].unsqueeze(2).to_broadcast(shape),
                                     tags[:, :, first:last].unsqueeze(3).to_broadcast(shape), ALU.mult)

        def proj_scale(eng, w):
            z = pz[:, w % 2, :]
            eng.wait_ge(pz_normed, w + 1)
            eng.tensor_tensor(z, z, ln2_g_bc, ALU.mult).then_inc(pz_scaled, 1)
            eng.wait_ge(pz_scaled, w + 1)
            eng.tensor_tensor(z, z, pos_bc[:, w, :], ALU.add).then_inc(pz_done, 1)

        def entry(n):
            return n if not isinstance(n, int) or 0 <= n < B else None

        def probsT_bank(b, g):
            return bank[2 + g] if closing(b) else bank[6 + g % 2]

        def logit_bank(r):
            return bank[7] if closing(r) else bank[1]

        def closing(b):
            return isinstance(b, int) and b >= B - 2

        def early(index, least):
            return isinstance(index, int) and index < least

        block = ctx.enter_context(nc.Block())

        @block.sync
        def _(sp):
            xv = x.rearrange("b c (h p) w -> c b h (p w)", p=PS)
            for c in range(C):
                sp.dma_start(px[:, c, :], xv[c]).then_inc(ld_x[c], 16)
            sp.wait_ge(ld_patch, PATCH_LOADS)
            for dst, vec in ((ln2_g_bc, ln2_g), (ln2_b_bc, ln2_b)):
                sp.dma_start(dst, vec.partition_broadcast(R)).then_inc(ld_z, 16)
            pos_v = pos_emb[0, 1:1 + G * G, :].rearrange("(a h w) e -> a h (w e)", a=1, w=G)
            sp.dma_start(pos_bc.rearrange("r w e -> r (w e)"), pos_v.to_broadcast([B, G, G * E]))\
               .then_inc(ld_z, 16)
            sp.dma_start(w_nat[:, 0:3 * EC, :], w_attn.rearrange("(m p) e -> p m e", p=128)).then_inc(ld_nat, 16)
            sp.dma_start(w_nat[:, 3 * EC:, :], w_proj.rearrange("(m p) e -> p m e", p=128)).then_inc(ld_nat, 16)
            sp.dma_start(cls_pos[:, 0, :], cls_token[0]).then_inc(ld_cls, 16)
            sp.dma_start(cls_pos[:, 1, :], pos_emb[0, 0:1, :]).then_inc(ld_cls, 16)
            sp.dma_start(gate_sb[:, :, :], gate_w.rearrange("(k p) x -> p k x", p=128)).then_inc(ld_const, 16)
            sp.dma_start(b1_nat[:, :], b1.rearrange("x (c p) -> (x c) p", p=128)).then_inc(ld_const, 16)
            sp.dma_start(rows[T - S:T, :, :], txt.rearrange("b s e -> s b e")).then_inc(ld_txt, 16)
            sp.wait_ge(cls_done, 1)
            sp.dma_start(rows[0:1, :, :], cls_pos[:, 0:1, :].to_broadcast([1, B, E])).then_inc(ld_txt, 16)
            for w in range(G + 1):
                if w < G:
                    sp.wait_ge(pz_done, w + 1)
                    sp.dma_start(patch_rows[w], pz[:, w % 2, :]).then_inc(st_patch[w % 2], 16)
                if w >= 1:
                    v = w - 1
                    sp.wait_ge(st_patch[v % 2], 16 * (v // 2 + 1))
                    sp.dma_start(rows[1 + v:2 + v + G * (G - 1):G, :, :],
                                 patch_rows[v].rearrange("(b h) e -> h b e", b=B)).then_inc(ld_tok, 16)
            sp.wait_ge(wT_copied, 4 * EC + 1)

            def load_expert(e):
                sp.dma_start(w1_sb[:, e], w1[e].rearrange("(k p) f -> p k f", p=128)).then_inc(ld_w[e], 16)
                sp.dma_start(w2_sb[:, e], w2[e].rearrange("(c p) d -> p c d", p=128)).then_inc(ld_w[e], 16)
            for e in range(X - 2):
                load_expert(e)

            def keep(b, par):
                sp.wait_ge(x2n_ready, b + 1)
                sp.dma_start(token_rows[bass.ds(b * T, T), :], x2[:, par, :]).then_inc(st_x2[par], 16)

            loop_by(2, sp, B - 1, keep)
            sp.wait_ge(pT_ps, NG * B)
            load_expert(X - 1)
            sp.wait_ge(pv_ps, B)
            load_expert(X - 2)
            keep(B - 1, (B - 1) % 2)
            sp.wait_ge(proj_ps, B)
            sp.dma_start(b2_bc, b2.partition_broadcast(128)).then_inc(ld_b2, 16)

        @block.gpsimd
        def _(pool):
            pool.memset(ident[:, :], 0.0).then_inc(pool_chain, 1)
            pool.memset(ident_bf[:, :], 0.0).then_inc(pool_chain, 1)
            pool.memset(mask_bf[:, :, :], 0.0).then_inc(pool_chain, 1)
            pool.memset(before[:, :], 1.0).then_inc(pool_chain, 1)
            pool.memset(ones_bf[:, :], 1.0).then_inc(pool_const, 1)
            pool.memset(chosen_bf[:, :, :], 0.0)
            pool.memset(ones_f[:, :], 1.0)
            pool.memset(ones_row, 1.0).then_inc(pool_const, 1)
            pool.memset(minus_half[:, :], -0.5)
            pool.memset(eps[:, :], LN_EPS).then_inc(pool_const, 1)
            pool.memset(head_of[:, :], 1.0).then_inc(pool_chain, 1)
            pool.wait_ge(pool_chain, 5)
            pool.affine_select(out=ident[:, :], in_=ident[:, :], compare_op=ALU.not_equal, fill=1.0,
                               base=0, pattern=[[-1, 128]], channel_multiplier=1).then_inc(pool_const, 1)
            pool.affine_select(out=ident_bf[:, :], in_=ident_bf[:, :], compare_op=ALU.not_equal, fill=1.0,
                               base=0, pattern=[[-1, T]], channel_multiplier=1).then_inc(pool_const, 1)
            pool.affine_select(out=mask_bf[:, :, :], in_=mask_bf[:, :, :], compare_op=ALU.is_ge, fill=MASKED,
                               base=0, pattern=[[0, HG], [-1, T]], channel_multiplier=1).then_inc(pool_const, 1)
            pool.affine_select(out=before[:, :], in_=before[:, :], compare_op=ALU.is_gt, fill=0.0,
                               base=0, pattern=[[1, T]], channel_multiplier=-1).then_inc(pool_const, 1)
            pool.affine_select(out=head_of[:, :], in_=head_of[:, :], compare_op=ALU.is_ge, fill=0.0,
                               base=0, pattern=[[-DK, H // EC]], channel_multiplier=1).then_inc(pool_chain, 1)
            pool.wait_ge(pool_chain, 6)
            pool.affine_select(out=head_of[:, :], in_=head_of[:, :], compare_op=ALU.is_ge, fill=0.0,
                               base=DK - 1, pattern=[[DK, H // EC]], channel_multiplier=-1).then_inc(pool_const, 1)
            pool.iota(expert_no[:, :], pattern=[[1, X]], base=0, channel_multiplier=0,
                      allow_small_or_imprecise_dtypes=True).then_inc(pool_const, 1)
            pool.iota(filled[:, :], pattern=[[SLOT, NFULL]], base=0, channel_multiplier=0,
                      allow_small_or_imprecise_dtypes=True).then_inc(pool_const, 1)
            pool.iota(blk_no[:, :], pattern=[[1, NBLK]], base=0, channel_multiplier=0,
                      allow_small_or_imprecise_dtypes=True).then_inc(pool_const, 1)
            pool.iota(slot_no[:, :], pattern=[[1, SLOT]], base=0, channel_multiplier=0,
                      allow_small_or_imprecise_dtypes=True).then_inc(pool_const, 1)
            pool.iota(tags[:, :, 0], pattern=[[1, B]], base=1, channel_multiplier=0,
                      allow_small_or_imprecise_dtypes=True).then_inc(pool_const, 1)
            pool.iota(tags[:, :, 1], pattern=[[0, B]], base=0, channel_multiplier=1,
                      allow_small_or_imprecise_dtypes=True).then_inc(pool_const, 1)

            def rstd(mv, rs, chain, base):
                n, m, _ = mv.shape
                pool.tensor_tensor(rs[:, :, 1], mv[:, :, 1], eps[0:n, 0:m], ALU.add).then_inc(chain, 1)
                pool.wait_ge(chain, base + 1)
                pool.tensor_tensor(rs[:, :, 0], rs[:, :, 1], minus_half[0:n, 0:m], ALU.pow).then_inc(chain, 1)
                pool.wait_ge(chain, base + 2)
                return pool.tensor_tensor(rs[:, :, 1], mv[:, :, 0], rs[:, :, 0], ALU.mult)

            def patch_rstd(w):
                pool.wait_ge(px_stats, w + 1)
                rstd(pmv[:, w:w + 1, :], prs[:, w:w + 1, :], px_pool, 2 * w).then_inc(px_rstd, 1)

            patch_rstd(0)
            patch_rstd(1)
            for w in range(G + 2):
                if w >= 2:
                    pool.wait_ge(pz_stats, w - 1)
                    rstd(zmv[:, w - 2:w - 1, :], zrs[:, w - 2:w - 1, :], pz_pool, 2 * (w - 2)).then_inc(pz_rstd, 1)
                if w + 2 < G:
                    patch_rstd(w + 2)
                if w == 1:
                    pool.wait_ge(ld_z, 16 * 3)
                    for v in range(G):
                        ins = pool.tensor_tensor(pos_bc[:, v, :], pos_bc[:, v, :], ln2_b_bc, ALU.add)
                    ins.then_inc(posb_done, 1)
                    pool.wait_ge(posb_done, 1)
                if 2 <= w < G + 1:
                    proj_scale(pool, w - 2)
            for par in range(2):
                pool.wait_ge(st_patch[par], 8 * G)
            pool.wait_ge(ld_txt, 32)
            pool.memset(v_aug[:, :, :, :], 1.0).then_inc(v_ones, 1)

            def ln1_rstd(n):
                g = slice(LN1_GROUPS[n].start, LN1_GROUPS[n].stop)
                pool.wait_ge(ln1_stats, n + 1)
                rstd(mv1[:, g, :], rs1[:, g, :], ln1_pool, 3 * n).then_inc(ln1_pool, 1)
                pool.wait_ge(ln1_pool, 3 * n + 3)

            def normalise(n, par):
                pool.tensor_tensor(xn[:, par, :], rows[:, n, :],
                                   rs1[:, n, 0:1].to_broadcast([T, E]), ALU.mult).then_inc(xn_scaled, 1)
                pool.wait_ge(xn_scaled, n - 1)
                pool.tensor_tensor(xn[:, par, :], xn[:, par, :],
                                   rs1[:, n, 1:2].to_broadcast([T, E]), ALU.subtract).then_inc(xn_ready, 1)

            for n in range(LN1_EARLY):
                ln1_rstd(n)

            def attention(s, par):
                ahead, f, r = entry(s + 2), entry(s), entry(s - 3)
                if r is not None:
                    pool.wait_ge(ln2_stats, r + 1)
                    rstd(mv2[:, 1 - par:2 - par, :], rs2[:, 1 - par:2 - par, :], ln2_pool, 2 * r).then_inc(ln2_rstd, 1)
                if f is not None:
                    pool.wait_ge(qk_split, f + 1)
                    for c in range(EC):
                        side_by_side(pool, heads_low, qk_low, c).then_inc(heads_lower, 1)
                if ahead is not None:
                    pool.wait_ge(xnT_ps, s + 1)
                    normalise(ahead, par)
                if isinstance(s, int) and s + LN1_EARLY < len(LN1_GROUPS):
                    ln1_rstd(s + LN1_EARLY)

            attention_steps(pool, attention)

            last_row = pool.to_reg(B * T - 1)

            def load_block(k):
                if k >= RING:
                    pool.wait_ge(blk_done, k - RING + 1)
                pool.indirect_dma_start(
                    out=blk_in[:, k % RING, :], out_offset=None, in_=token_rows[:, :],
                    in_offset=bass.IndirectOffsetOnAxis(ap=from_row[:, k:k + 1].bitcast(U32), axis=0))\
                    .then_inc(ld_blk[k % RING], 16)

            def store_block(k):
                pool.wait_ge(blk_done, k + 1)
                pool.indirect_dma_start(
                    out=out_rows, out_offset=bass.IndirectOffsetOnAxis(ap=to_row[:, k:k + 1].bitcast(U32), axis=0),
                    in_=blk_out[:, k % 2, :], in_offset=None,
                    bounds_check=last_row, oob_is_err=False).then_inc(st_out[k % 2], 16)

            def lower_act(k):
                pool.wait_ge(act_upper, k + 1)
                pool.tensor_tensor(act_low[:, :, :], actT[:, k % 2], act_up[:, :, :].bitcast(F32), ALU.subtract)\
                    .then_inc(act_split, 1)

            pool.wait_ge(in_blk_done, 1)
            tag(pool, 0, 2).then_inc(tokens_tagged, 1)
            for par in range(2):
                pool.wait_ge(st_x2[par], 8 * B)
            pool.wait_ge(from_row_done, 1)
            for k in range(RING):
                load_block(k)
            pool.wait_ge(to_row_done, 1)
            lower_act(1)
            for k in range(NBLK):
                if k + RING < NBLK:
                    load_block(k + RING)
                if k + 2 < NBLK - 1:
                    lower_act(k + 2)
                store_block(k)
            for par in range(2):
                pool.wait_ge(st_out[par], 16 * (NBLK // 2))

        @block.scalar
        def _(act):
            with nc.allow_non_contiguous_dma(reason="two short vectors, once"):
                for n, vec in enumerate((ln1_g, ln1_b)):
                    for u in range(PC // C):
                        act.dma_start(pg[:, n, :, u],
                                      vec.rearrange("(u k c) -> u k c", u=PC // C, c=C)[u])\
                            .then_inc(ld_patch, 16)
            for u in range(PC // C):
                act.dma_start(w_patch_sb.rearrange("k (c u) e -> k u c e", c=C)[:, u],
                              w_patch.rearrange("(u k c) e -> u k c e", u=PC // C, c=C)[u]).then_inc(ld_patch, 16)
            act.dma_start(b_patch_sb, b_patch.partition_broadcast(1)).then_inc(ld_patch, 16)

            act.wait_ge(pool_const, 3)
            act.activation(unused[:, :], eps[0:1, 0:1], ACT.Identity)

            act.wait_ge(ld_patch, PATCH_LOADS)

            def patch_evict(w, par):
                act.wait_ge(px_T, w + 1)
                if not early(w, 2):
                    act.wait_ge(pz_ps, w - 1)
                for c in range(PC):
                    src = bank[2 * par + c // 3][:, (c % 3) * R:(c % 3 + 1) * R]
                    ins = act.activation(pxT[:, par, c, :], src, ACT.Identity,
                                         bias=pg[:, 1, c // 2, c % 2:c % 2 + 1],
                                         scale=pg[:, 0, c // 2, c % 2:c % 2 + 1])
                ins.then_inc(px_Tcopied, 1)

            loop_by(2, act, G, patch_evict)

            for n in range(3 * EC + EC):
                act.wait_ge(wT_ps, n + 1)
                dst = w_attnT[:, :, n * 128:(n + 1) * 128] if n < 3 * EC else \
                    w_projT[:, :, (n - 3 * EC) * 128:(n - 3 * EC + 1) * 128]
                act.activation(dst, bank[6][:, 0:EC * 128].rearrange("p (k n) -> p k n", k=EC),
                               ACT.Copy).then_inc(wT_copied, 1)
            act.wait_ge(wT_ps, 4 * EC + 1)
            act.activation(b1T[:, :], bank[6][:, 0:X * FC], ACT.Copy).then_inc(wT_copied, 1)
            act.wait_ge(v_ones, 1)

            def copy_xnT(n, par):
                act.wait_ge(xnT_ps, n + 1)
                if not early(n, 2):
                    act.wait_ge(v_ps, n - 1)
                act.activation(xnT[:, par, :, :], bank[7][:, 0:EC * T].rearrange("p (k t) -> p k t", k=EC),
                               ACT.Copy).then_inc(xnT_copied, 1)

            copy_xnT(0, 0)

            def attention(s, par):
                n, f, e, b, r = entry(s + 1), entry(s), entry(s - 1), entry(s - 2), entry(s - 3)
                A, BB = bank[0], bank[1]

                def copy_pT(g):
                    act.wait_ge(pT_ps, NG * b + g + 1)
                    if g == 0 and not early(b, 1):
                        act.wait_ge(pv_ps, b)
                    act.activation(probsT[:, HG * g:HG * (g + 1), :],
                                   probsT_bank(b, g)[0:T, 0:HG * T].rearrange("p (h t) -> p h t", h=HG),
                                   ACT.Copy).then_inc(pT_copied, 1)

                def exponentiate(g):
                    act.wait_ge(shifted, NG * e + g + 1)
                    p = probs[:, 1 - par, HG * g:HG * (g + 1), :]
                    act.activation(p, p, ACT.Exp, scale=float(DK) ** -0.5).then_inc(exp_done, 1)

                if b is not None:
                    copy_pT(0)
                    copy_pT(1)
                if f is not None:
                    act.wait_ge(qk_ps, f + 1)
                    if not early(f, 1):
                        act.wait_ge(scores_ps, NG * f)
                    act.activation(qk_up, A[:, 0:2 * EC * T].rearrange("p (n k t) -> p n k t", n=2, k=EC),
                                   ACT.Copy).then_inc(qk_upper, 1)
                if b is not None:
                    copy_pT(2)
                    copy_pT(3)
                ending = isinstance(e, int) and e == B - 1
                if e is not None:
                    for g in range(NG if ending else 2):
                        exponentiate(g)
                if n is not None:
                    copy_xnT(n, 1 - par)
                if f is not None:
                    act.wait_ge(v_ps, f + 1)
                    if not early(f, 2):
                        act.wait_ge(pv_ps, f - 1)
                    act.activation(v_aug[:, par, :, 0:DK],
                                   BB[0:T, 0:E].rearrange("p (h d) -> p h d", h=H), ACT.Copy)\
                       .then_inc(v_copied, 1)
                if r is not None:
                    act.wait_ge(x2T_ps, r + 1)
                    if not early(r, 1):
                        act.wait_ge(logit_ps, r)
                    act.activation(x2T[:, :, :], A[:, 0:EC * T].rearrange("p (k t) -> p k t", k=EC),
                                   ACT.Copy).then_inc(x2T_copied, 1)
                if e is not None and not ending:
                    exponentiate(2)
                if b is not None:
                    act.wait_ge(oT_ps, b + 1)
                    if not early(b, 1):
                        act.wait_ge(proj_ps, b)
                    act.activation(oT[:, :, :], BB[:, 0:EC * T].rearrange("p (k t) -> p k t", k=EC),
                                   ACT.Copy).then_inc(oT_copied, 1)
                if e is not None and not ending:
                    exponentiate(3)

            attention_steps(act, attention)

            for n, part in enumerate((slice(0, B - 1), slice(B - 1, B))):
                act.wait_ge(l_shifted, n + 1)
                act.activation(lexp[:, part, :], lexp[:, part, :], ACT.Exp).then_inc(l_exp, 1)
            act.activation(unused[:, :], ones_f[0:1, 0:1], ACT.Gelu)

            act.wait_ge(blk_ex_done, 1)

            def upper_w2(k, e):
                for c in range(0, FC, FC // 2):
                    part = slice(c, c + FC // 2)
                    act.activation(w2_up[:, part, :], w2_sb[:, bass.ds(e, 1), part, :], ACT.Copy)\
                       .then_inc(w2_upper, 1)

            def expert(k, par, last=False):
                e = act.value_load(blk_ex[0:1, bass.ds(k, 1)], min_val=0, max_val=X - 1)
                if early(k, 1):
                    upper_w2(k, e)
                for c in range(FC):
                    if c % 4 == 0:
                        act.wait_ge(hid_ps, 2 * k + c // 4 + 1)
                        if not early(k, 2):
                            act.wait_ge(act_split, k - 1)
                    ins = act.activation(actT[:, par, c, :],
                                         bank[2 * par + c // 4][:, c % 4 * 128:(c % 4 + 1) * 128],
                                         ACT.Gelu, bias=b1T[:, bass.ds(e * FC + c, 1)])
                    if c % 4 == 3:
                        ins.then_inc(gelu_done, 1)
                if not early(k, 1) and not last:
                    act.wait_ge(y_ps, k)
                    upper_w2(k, e)

            for e in range(X):
                act.wait_ge(ld_w[e], 32)
            loop_by(2, act, NBLK - 1, expert)
            expert(NBLK - 1, 1, last=True)

        @block.tensor
        def _(pe):
            pe.wait_ge(pool_const, 7)

            def patch_T(w, par):
                pe.wait_ge(px_norm, w + 1)
                if not early(w, 2):
                    pe.wait_ge(px_Tcopied, w - 1)
                for c in range(PC):
                    ins = pe.transpose(bank[2 * par + c // 3][:, (c % 3) * R:(c % 3 + 1) * R],
                                       pxn[:, par, c * 128:(c + 1) * 128], ident[0:R, 0:R])
                ins.then_inc(px_T, 1)

            def patch_mm(w, par):
                pe.wait_ge(px_Tcopied, w + 1)
                if not early(w, 2):
                    pe.wait_ge(pz_normed, w - 1)
                pe.matmul(bank[4 + par][0:R, 0:E], ones_row, b_patch_sb, start=True, stop=False)
                for c in range(PC):
                    ins = pe.matmul(bank[4 + par][0:R, 0:E], pxT[:, par, c, :], w_patch_sb[:, c, :],
                                    start=False, stop=(c == PC - 1))
                ins.then_inc(pz_ps, 1)

            patch_T(0, 0)
            pe.wait_ge(ld_patch, PATCH_LOADS)
            patch_T(1, 1)
            patch_mm(0, 0)
            with pe.Fori(1, G // 2) as i:
                patch_T(2 * i, 0)
                patch_mm(2 * i - 1, 1)
                patch_T(2 * i + 1, 1)
                patch_mm(2 * i, 0)
            patch_mm(G - 1, 1)

            for n in range(4 * EC):
                if n == 0:
                    pe.wait_ge(ld_nat, 32)
                if n >= 1:
                    pe.wait_ge(wT_copied, n)
                for k in range(EC):
                    ins = pe.transpose(bank[6][:, k * 128:(k + 1) * 128],
                                       w_nat[:, n, k * 128:(k + 1) * 128], ident[:, :])
                ins.then_inc(wT_ps, 1)
            pe.wait_ge(wT_copied, 4 * EC)
            pe.wait_ge(ld_const, 32)
            pe.transpose(bank[6][:, 0:X * FC], b1_nat[:, :], ident[0:X * FC, 0:X * FC]).then_inc(wT_ps, 1)
            pe.wait_ge(wT_copied, 4 * EC + 1)

            def norm_T(n, par):
                pe.wait_ge(xn_ready, n + 1)
                for k in range(EC):
                    ins = pe.transpose(bank[7][:, k * T:(k + 1) * T], xn[:, par, k * 128:(k + 1) * 128],
                                       ident[0:T, 0:T])
                ins.then_inc(xnT_ps, 1)

            norm_T(0, 0)
            pe.wait_ge(px_Tcopied, G)
            pe.wait_ge(pz_normed, G)

            picks = chosen_bf[:, :, :].rearrange("p b x -> p (b x)")

            def early_ranks():
                pe.wait_ge(chosen_done, 1)
                pe.matmul(bank[4][0:T, 0:B * X], before[:, :], picks, start=True, stop=False)
                for d in range(1, B):
                    pe.matmul(bank[4][0:T, d * X:B * X], ones_bf[:, :], picks[:, 0:(B - d) * X],
                              start=False, stop=False)
                pe.matmul(bank[5][0:T, 0:B * X], ones_bf[:, :], picks, start=True, stop=False)\
                  .then_inc(early_ranks_ps, 1)

            def attention(s, par):
                n, f, b, r = entry(s + 1), entry(s), entry(s - 2), entry(s - 3)
                A, BB = bank[0], bank[1]

                def probs_T(g, b=b, par=par):
                    pe.wait_ge(exp_done, NG * b + g + 1)
                    if closing(b):
                        pe.wait_ge(shifted, NG * (B - 1) + g + 1)
                    elif g >= 2:
                        pe.wait_ge(pT_copied, NG * b + g - 1)
                    elif g == 1 and f is not None:
                        pe.wait_ge(xnT_copied, f + 1)
                    elif g == 0 and not early(b, 1):
                        pe.wait_ge(o_done, b)
                    for j in range(HG):
                        ins = pe.transpose(probsT_bank(b, g)[0:T, j * T:(j + 1) * T],
                                           probs[:, par, HG * g + j, :], ident[0:T, 0:T])
                    ins.then_inc(pT_ps, 1)

                def weighted_v(g):
                    if closing(b):
                        pe.wait_ge(pT_copied, NG * b + g + 1)
                    for h in range(HG * g, HG * (g + 1)):
                        ins = pe.matmul(bank[6][0:T, h * (DK + 1):(h + 1) * (DK + 1)], probsT[:, h, :],
                                        v_aug[:, par, h, :], start=True, stop=True)
                    if g == NG - 1:
                        ins.then_inc(pv_ps, 1)

                def mask(g):
                    if not early(f, 1):
                        pe.wait_ge(shifted, NG * (f - 1) + g + 1)
                    pe.matmul(bank[2 + g][0:T, 0:HG * T], ident_bf[:, :],
                              mask_bf[:, :, :].rearrange("p h t -> p (h t)"), start=True, stop=False)

                def scores(g):
                    c, h = HG * g // (H // EC), HG * g % (H // EC)
                    pe.wait_ge(heads_lower, EC * f + c + 1)
                    out = bank[2 + g][0:T, 0:HG * T]
                    for n, (q, k) in enumerate(((qk_up, heads_up), (qk_low, heads_up), (qk_up, heads_low))):
                        ins = pe.matmul(out, q[:, 0, c, :], k[:, c, h:h + HG, :].rearrange("p h t -> p (h t)"),
                                        start=False, stop=(n == 2))
                    ins.then_inc(scores_ps, 1)

                fills = isinstance(s, int) and s == B
                filled_before = isinstance(s, int) and s == B + 1
                if b is not None and not filled_before:
                    probs_T(0)
                    probs_T(1)
                if f is not None:
                    pe.wait_ge(xnT_copied, f + 1)
                    if not early(f, 4):
                        pe.wait_ge(x2T_copied, f - 3)
                    elif f >= 1:
                        pe.wait_ge(qk_split, f)
                    for m in range(2 * EC):
                        for k in range(EC):
                            ins = pe.matmul(A[:, m * T:(m + 1) * T], w_attnT[:, k, m * 128:(m + 1) * 128],
                                            xnT[:, par, k, :], start=(k == 0), stop=(k == EC - 1))
                    ins.then_inc(qk_ps, 1)
                if b is not None and not filled_before:
                    probs_T(2)
                    probs_T(3)
                if f is not None:
                    if not early(f, 3):
                        pe.wait_ge(resid_done, f - 2)
                    elif f >= 1:
                        pe.wait_ge(v_copied, f)
                    if not early(f, 4):
                        pe.wait_ge(logit_kept, f - 3)
                    for k in range(EC):
                        ins = pe.matmul(BB[0:T, 0:E], xnT[:, par, k, :], w_attnT[:, k, 2 * E:3 * E],
                                        start=(k == 0), stop=(k == EC - 1))
                    ins.then_inc(v_ps, 1)
                    mask(0)
                    mask(1)
                if b is not None:
                    if not closing(b):
                        pe.wait_ge(pT_copied, NG * (b + 1))
                    pe.wait_ge(v_copied, b + 1)
                    weighted_v(0)
                if f is not None:
                    mask(2)
                    mask(3)
                if b is not None:
                    weighted_v(1)
                if n is not None:
                    norm_T(n, 1 - par)
                if b is not None:
                    weighted_v(2)
                if f is not None:
                    pe.wait_ge(heads_upper, f + 1)
                    scores(0)
                if b is not None:
                    weighted_v(3)
                if f is not None:
                    scores(1)
                if r is not None:
                    pe.wait_ge(x2n_ready, r + 1)
                    if f is None:
                        pe.wait_ge(x2T_copied, r)
                    for k in range(EC):
                        ins = pe.transpose(A[:, k * T:(k + 1) * T], x2[:, 1 - par, k * 128:(k + 1) * 128],
                                           ident[0:T, 0:T])
                    ins.then_inc(x2T_ps, 1)
                if f is not None:
                    scores(2)
                if fills:
                    probs_T(0, b + 1, 1 - par)
                    probs_T(1, b + 1, 1 - par)
                if b is not None:
                    pe.wait_ge(o_done, b + 1)
                    if f is not None:
                        pe.wait_ge(v_copied, f + 1)
                    else:
                        pe.wait_ge(resid_done, b)
                        pe.wait_ge(logit_kept, b - 1)
                    for k in range(EC):
                        ins = pe.transpose(BB[:, k * T:(k + 1) * T], o_sb[:, k * 128:(k + 1) * 128],
                                           ident[0:T, 0:T])
                    ins.then_inc(oT_ps, 1)
                if f is not None:
                    scores(3)
                if fills:
                    probs_T(2, b + 1, 1 - par)
                    probs_T(3, b + 1, 1 - par)
                if b is not None:
                    pe.wait_ge(oT_copied, b + 1)
                if r is not None:
                    pe.wait_ge(x2T_copied, r + 1)
                    if b is None:
                        pe.wait_ge(logit_kept, r)
                    for k in range(EC):
                        ins = pe.matmul(logit_bank(r)[0:T, E:E + X], x2T[:, k, :], gate_sb[:, k, :],
                                        start=(k == 0), stop=(k == EC - 1))
                    ins.then_inc(logit_ps, 1)
                if b is not None:
                    for k in range(EC):
                        ins = pe.matmul(BB[0:T, 0:E], oT[:, k, :], w_projT[:, k, :],
                                        start=(k == 0), stop=(k == EC - 1))
                    ins.then_inc(proj_ps, 1)
                    if isinstance(b, int) and b == B - 1:
                        early_ranks()

            attention_steps(pe, attention)

            pe.wait_ge(chosen_done, 2)
            last = slice((B - 1) * X, B * X)
            pe.matmul(bank[4][0:T, last], before[:, :], picks[:, last], start=False, stop=True)
            pe.matmul(bank[5][0:T, last], ones_bf[:, :], picks[:, last], start=False, stop=True).then_inc(rank_ps, 1)

            def tell(out, first, last):
                for b in range(B):
                    if first == 0 and b % (B // 2) == 0:
                        pe.wait_ge(in_slot_done, 2 * b // B + 1)
                    ins = pe.matmul(out, in_slot[:, b, :], tagged[:, b, first:last, :].rearrange("p f k -> p (f k)"),
                                    start=(b == 0), stop=(b == B - 1))
                return ins

            pe.wait_ge(tokens_tagged, 1)
            tell(bank[2][:, 0:2 * NBLK], 0, 2).then_inc(tokens_ps, 1)
            pe.wait_ge(weights_tagged, 1)
            tell(bank[7][:, 0:PIECES * NBLK], 2, 2 + PIECES).then_inc(weights_ps, 1)

            pe.wait_ge(blk_ex_done, 1)

            def block_T(k, slot):
                pe.wait_ge(ld_blk[slot], 16 // RING * (k - slot) + 16)
                if not early(k, 1):
                    pe.wait_ge(blkT_copied, k)
                for c in range(EC):
                    ins = pe.transpose(bank[6][:, c * 128:(c + 1) * 128],
                                       blk_in[:, slot, c * 128:(c + 1) * 128], ident[:, :])
                ins.then_inc(blkT_ps, 1)

            def hidden(k, par):
                pe.wait_ge(blkT_copied, k + 1)
                pe.wait_ge(w1_copied, k + 1)
                for n in range(FC // 4):
                    if not early(k, 2):
                        pe.wait_ge(gelu_done, 2 * (k - 2) + n + 1)
                    for j in range(4):
                        f = 4 * n + j
                        for c in range(EC):
                            ins = pe.matmul(bank[2 * par + n][:, j * 128:(j + 1) * 128],
                                            w1_now[:, par, c, f * 128:(f + 1) * 128], blkT[:, par, c, :],
                                            start=(c == 0), stop=(c == EC - 1))
                    ins.then_inc(hid_ps, 1)

            def down(k, par):
                pe.wait_ge(act_split, k + 1)
                if not early(k, 2):
                    pe.wait_ge(y_biased, k - 1)
                for c in range(FC):
                    if c % (FC // 2) == 0:
                        pe.wait_ge(w2_split, 2 * k + c // (FC // 2) + 1)
                    for n, (a, w) in enumerate(((act_up, w2_up), (act_up, w2_low), (act_low, w2_up))):
                        ins = pe.matmul(bank[4 + par][:, 0:E], a[:, c, :], w[:, c, :],
                                        start=(c == 0 and n == 0), stop=(c == FC - 1 and n == 2))
                ins.then_inc(y_ps, 1)

            def down_whole(k, par):
                pe.wait_ge(w2_copied, 1)
                pe.wait_ge(y_biased, k - 1)
                for c in range(FC):
                    if c % 4 == 0:
                        pe.wait_ge(gelu_done, 2 * k + c // 4 + 1)
                    ins = pe.matmul(bank[4 + par][:, 0:E], actT[:, par, c, :], w2_last[:, c, :],
                                    start=(c == 0), stop=(c == FC - 1))
                ins.then_inc(y_ps, 1)

            def turn(k, slot, more=True):
                par = slot % 2
                hidden(k + 1, 1 - par)
                if more:
                    block_T(k + 2, (slot + 2) % RING)
                down(k, par)

            block_T(0, 0)
            block_T(1, 1)
            hidden(0, 0)
            loop_by(RING, pe, NBLK - 2, turn)
            turn(NBLK - 2, 0, more=False)
            down_whole(NBLK - 1, 1)

        @block.vector
        def _(dve):
            patches = px.rearrange("r c (p w q) -> r c w p q", p=PS, w=G)

            def patch_stats(w):
                for c in range(C):
                    if w == 0:
                        dve.wait_ge(ld_x[c], 16)
                    ins = dve.bn_stats(px_six[:, w, c, :], patches[:, c, w])
                ins.then_inc(p_chain, 1)
                dve.wait_ge(p_chain, w + 1)
                dve.bn_aggr(pmv[:, w, :], px_six[:, w, :, :]).then_inc(px_stats, 1)

            def patch_norm(w):
                dve.wait_ge(px_rstd, w + 1)
                if w >= 2:
                    dve.wait_ge(px_T, w - 1)
                dve.tensor_scalar(pxn[:, w % 2, :].rearrange("r (c p q) -> r c p q", c=C, p=PS),
                                  patches[:, :, w], prs[:, w, 0:1], prs[:, w, 1:2],
                                  ALU.mult, ALU.subtract).then_inc(px_norm, 1)

            def proj_stats(w):
                dve.wait_ge(pz_ps, w + 1)
                dve.bn_stats(pz_six[:, w, :], bank[4 + w % 2][0:R, 0:E]).then_inc(pz_chain, 1)
                dve.wait_ge(pz_chain, w + 1)
                dve.bn_aggr(zmv[:, w, :], pz_six[:, w, :]).then_inc(pz_stats, 1)

            def proj_norm(w):
                dve.wait_ge(pz_rstd, w + 1)
                if w >= 2:
                    dve.wait_ge(st_patch[w % 2], 16 * (w // 2))
                dve.tensor_scalar(pz[:, w % 2, :], bank[4 + w % 2][0:R, 0:E], zrs[:, w, 0:1], zrs[:, w, 1:2],
                                  ALU.mult, ALU.subtract).then_inc(pz_normed, 1)

            patch_stats(0)
            patch_stats(1)
            for w in range(G + 2):
                if w < G:
                    patch_norm(w)
                if w >= 2:
                    proj_stats(w - 2)
                if w + 2 < G:
                    patch_stats(w + 2)
                if w >= 2:
                    proj_norm(w - 2)
                if w == 2:
                    dve.wait_ge(ld_cls, 32)
                    dve.tensor_tensor(cls_pos[:, 0, :], cls_pos[:, 0, :], cls_pos[:, 1, :], ALU.add)\
                       .then_inc(cls_done, 1)

            dve.wait_ge(posb_done, 1)
            proj_scale(dve, G - 1)

            dve.wait_ge(ld_txt, 32)
            dve.wait_ge(ld_tok, 16 * G)

            def ln1_statistics(n):
                entries = LN1_GROUPS[n]
                for b in entries:
                    ins = dve.bn_stats(six1[:, b, :], rows[:, b, :])
                ins.then_inc(ln1_chain, 1)
                dve.wait_ge(ln1_chain, n + 1)
                for b in entries:
                    ins = dve.bn_aggr(mv1[:, b, :], six1[:, b, :])
                ins.then_inc(ln1_stats, 1)

            for n in range(LN1_EARLY):
                ln1_statistics(n)
            dve.wait_ge(ln1_pool, 3)
            for b in LN1_GROUPS[0]:
                dve.tensor_scalar(xn[:, b, :], rows[:, b, :], rs1[:, b, 0:1], rs1[:, b, 1:2],
                                  ALU.mult, ALU.subtract).then_inc(xn_ready, 1)

            steps = [0]

            def then(*results):
                for ins in results:
                    ins.then_inc(r_chain, 1)
                steps[0] += len(results)
                dve.wait_ge(r_chain, steps[0])

            def choose(first, last):
                n = last - first
                over_x = lmax[:, first:last].unsqueeze(2).to_broadcast([T, n, X])
                lg, key, pick = logits[:, first:last, :], lkey[:, first:last, :], chosen[:, first:last, :]
                then(dve.tensor_reduce(lmax[:, first:last], lg, AX.X, ALU.max))
                dve.tensor_tensor(lexp[:, first:last, :], lg, over_x, ALU.subtract).then_inc(l_shifted, 1)
                then(dve.tensor_tensor(key, lg, over_x, ALU.is_equal))
                then(dve.scalar_tensor_tensor(out=key, in0=key, scalar=float(-X),
                                              in1=expert_no[:, :].unsqueeze(1).to_broadcast([T, n, X]),
                                              op0=ALU.mult, op1=ALU.add))
                then(dve.tensor_reduce(lfirst[:, first:last], key, AX.X, ALU.min))
                then(dve.tensor_tensor(pick, key, lfirst[:, first:last].unsqueeze(2).to_broadcast([T, n, X]),
                                       ALU.is_equal))
                if first:
                    dve.wait_ge(early_ranks_ps, 1)
                dve.tensor_copy(chosen_bf[:, first:last, :], pick).then_inc(chosen_done, 1)

            dve.wait_ge(pool_const, 14)

            def attention(s, par):
                f, b, r = entry(s), entry(s - 2), entry(s - 3)
                A, BB = bank[0], bank[1]
                if f is not None:
                    dve.wait_ge(qk_upper, f + 1)
                    if not early(f, 1):
                        dve.wait_ge(scores_ps, NG * f)
                    dve.tensor_tensor(qk_low, A[:, 0:2 * EC * T].rearrange("p (n k t) -> p n k t", n=2, k=EC),
                                      qk_up.bitcast(F32), ALU.subtract).then_inc(qk_split, 1)
                    for c in range(EC):
                        ins = side_by_side(dve, heads_up, qk_up, c)
                    ins.then_inc(heads_upper, 1)
                if r is not None:
                    dve.wait_ge(ln2_rstd, r + 1)
                    if not early(r, 2):
                        dve.wait_ge(x2T_ps, r - 1)
                    dve.tensor_scalar(x2[:, 1 - par, 0:E], x2[:, 1 - par, RES:RES + E], rs2[:, 1 - par, 0:1],
                                      rs2[:, 1 - par, 1:2], ALU.mult, ALU.subtract).then_inc(x2n_ready, 1)

                early_choice = isinstance(r, int) and r == B - 2

                def keep_logits():
                    dve.wait_ge(logit_ps, r + 1)
                    dve.tensor_copy(logits[:, r, :], logit_bank(r)[0:T, E:E + X]).then_inc(logit_kept, 1)

                def largest(g):
                    dve.wait_ge(scores_ps, NG * f + g + 1)
                    dve.tensor_reduce(smax[:, par, HG * g:HG * (g + 1)],
                                      bank[2 + g][0:T, 0:HG * T].rearrange("p (h t) -> p h t", h=HG),
                                      AX.X, ALU.max).then_inc(max_done, 1)

                def subtract_largest(g):
                    heads = slice(HG * g, HG * (g + 1))
                    dve.wait_ge(max_done, NG * f + g + 1)
                    if g == 0 and not early(f, 2):
                        dve.wait_ge(pT_ps, NG * (f - 1))
                    dve.tensor_tensor(probs[:, par, heads, :],
                                      bank[2 + g][0:T, 0:HG * T].rearrange("p (h t) -> p h t", h=HG),
                                      smax[:, par, heads].unsqueeze(2).to_broadcast([T, HG, T]),
                                      ALU.subtract).then_inc(shifted, 1)

                if isinstance(s, int) and s + LN1_EARLY < len(LN1_GROUPS):
                    ln1_statistics(s + LN1_EARLY)
                if f is not None:
                    largest(0)
                if b is not None:
                    ov = bank[6][0:T, 0:H * (DK + 1)].rearrange("p (h d) -> p h d", h=H)
                    dve.wait_ge(pv_ps, b + 1)
                    dve.reciprocal(rsum[:, :], ov[:, :, DK]).then_inc(rsum_done, 1)
                    dve.wait_ge(rsum_done, b + 1)
                    if not early(b, 1):
                        dve.wait_ge(oT_ps, b)
                    dve.tensor_tensor(o_sb.rearrange("p (h d) -> p h d", h=H), ov[:, :, 0:DK],
                                      rsum[:, :].unsqueeze(2).to_broadcast([T, H, DK]), ALU.mult)\
                       .then_inc(o_done, 1)
                if early_choice:
                    keep_logits()
                    dve.wait_ge(logit_kept, B - 1)
                    choose(0, B - 1)
                if f is not None:
                    largest(1)
                    subtract_largest(0)
                    largest(2)
                    subtract_largest(1)
                    largest(3)
                    subtract_largest(2)
                    subtract_largest(3)
                if b is not None:
                    res = x2[:, par, RES:RES + E]
                    dve.wait_ge(proj_ps, b + 1)
                    if not early(b, 2):
                        dve.wait_ge(st_x2[par], 8 * (b - par))
                    dve.tensor_tensor(res, BB[0:T, 0:E], rows[:, b, :], ALU.add).then_inc(resid_done, 1)
                    dve.wait_ge(resid_done, b + 1)
                    dve.bn_stats(six2[:, par, :], res).then_inc(ln2_chain, 1)
                    dve.wait_ge(ln2_chain, b + 1)
                if r is not None and not early_choice:
                    keep_logits()
                if b is not None:
                    dve.bn_aggr(mv2[:, par, :], six2[:, par, :]).then_inc(ln2_stats, 1)

            attention_steps(dve, attention)

            def weight_piece(n):
                return dve.tensor_copy(tags[:, :, 2 + n], weight[:, :])

            def rest_of_weight(n):
                return dve.tensor_tensor(weight[:, :], weight[:, :], tags[:, :, 2 + n], ALU.subtract)

            dve.wait_ge(logit_kept, B)
            choose(B - 1, B)
            dve.wait_ge(l_exp, 2)
            then(dve.tensor_reduce(lsum[:, :], lexp[:, :, :], AX.X, ALU.add))
            dve.wait_ge(rank_ps, 1)
            then(dve.tensor_reduce(count[:, :], bank[5][0:T, 0:B * X].rearrange("p (b x) -> p x b", b=B),
                                   AX.X, ALU.add),
                 dve.reciprocal(weight[:, :], lsum[:, :]))
            then(dve.tensor_tensor(many[:, :, :], count[:, :].unsqueeze(2).to_broadcast([T, X, NFULL]),
                                   filled[:, :].unsqueeze(1).to_broadcast([T, X, NFULL]), ALU.is_gt),
                 weight_piece(0))
            then(dve.tensor_reduce(nblk[:, :], many[:, :, :], AX.X, ALU.add), rest_of_weight(0))
            then(dve.tensor_tensor_scan(blk_end[:, :], ones_f[:, :], nblk[:, :], 0.0, ALU.mult, ALU.add),
                 weight_piece(1))
            then(dve.tensor_tensor(start[:, :], blk_end[:, :], nblk[:, :], ALU.subtract), rest_of_weight(1))
            then(dve.scalar_tensor_tensor(out=slot_of[:, :, :], in0=start[:, :].unsqueeze(1).to_broadcast([T, B, X]),
                                          scalar=float(SLOT),
                                          in1=bank[4][0:T, 0:B * X].rearrange("p (b x) -> p b x", b=B),
                                          op0=ALU.mult, op1=ALU.add),
                 weight_piece(2))
            then(dve.tensor_tensor(slot_of[:, :, :], slot_of[:, :, :], chosen[:, :, :], ALU.mult))
            then(dve.tensor_reduce(pos_f[:, :], slot_of[:, :, :], AX.X, ALU.add))
            then(dve.tensor_copy(pos[:, :], pos_f[:, :]))
            dve.tensor_scalar(slot_i[:, 0, :], pos[:, :], SLOT - 1, None, ALU.bitwise_and)
            then(dve.tensor_scalar(slot_i[:, 1, :], pos[:, :], SLOT.bit_length() - 1, None, ALU.arith_shift_right))
            then(dve.tensor_copy(slot_f[:, :, :], slot_i[:, :, :]))
            dve.tensor_tensor(in_blk[:, :, :], slot_f[:, 1, :].unsqueeze(2).to_broadcast([T, B, NBLK]),
                              blk_no[:, :].unsqueeze(1).to_broadcast([T, B, NBLK]), ALU.is_equal)\
               .then_inc(in_blk_done, 1)
            for half in range(2):
                n = B // 2
                part = slice(half * n, (half + 1) * n)
                dve.tensor_tensor(in_slot[:, part, :], slot_f[:, 0, part].unsqueeze(2).to_broadcast([T, n, SLOT]),
                                  slot_no[:, :].unsqueeze(1).to_broadcast([T, n, SLOT]), ALU.is_equal)\
                   .then_inc(in_slot_done, 1)
            then(dve.tensor_tensor(blk_cmp[:, :, :], blk_no[0:1, :].unsqueeze(2).to_broadcast([1, NBLK, X]),
                                   blk_end[0:1, :].unsqueeze(1).to_broadcast([1, NBLK, X]), ALU.is_ge))
            then(dve.tensor_reduce(blk_ex_f[:, :], blk_cmp[:, :, :], AX.X, ALU.add))
            dve.tensor_scalar(blk_ex[:, :], blk_ex_f[:, :], float(X - 1), None, ALU.min).then_inc(blk_ex_done, 1)
            dve.wait_ge(tokens_ps, 1)
            then(dve.tensor_copy(token_of[:, :], bank[2][:, 0:NBLK]))
            then(dve.scalar_tensor_tensor(out=token_of[:, :], in0=token_of[:, :], scalar=float(T),
                                          in1=bank[2][:, NBLK:2 * NBLK], op0=ALU.mult, op1=ALU.add))
            dve.tensor_scalar(from_row[:, :], token_of[:, :], float(-T), 0.0, ALU.add, ALU.max)\
               .then_inc(from_row_done, 1)
            dve.wait_ge(in_blk_done, 1)
            tag(dve, 2, 2 + PIECES).then_inc(weights_tagged, 1)
            then(dve.tensor_scalar(vacant[:, :], token_of[:, :], float(T), float(NOBODY), ALU.is_lt, ALU.mult))
            then(dve.tensor_tensor(vacant[:, :], vacant[:, :], token_of[:, :], ALU.add))
            dve.tensor_scalar(to_row[:, :], vacant[:, :], float(-T), None, ALU.add).then_inc(to_row_done, 1)
            dve.wait_ge(blk_ex_done, 1)

            def copy_block(k, par):
                dve.wait_ge(blkT_ps, k + 1)
                if not early(k, 2):
                    dve.wait_ge(hid_ps, 2 * (k - 1))
                dve.tensor_copy(blkT[:, par, :, :], bank[6][:, 0:E].rearrange("p (c t) -> p c t", c=EC))\
                   .then_inc(blkT_copied, 1)

            def expert_of(k, known):
                base, off = k
                if off not in known:
                    known[off] = dve.value_load(blk_ex[0:1, bass.ds(base + off, 1)], min_val=0, max_val=X - 1)
                return known[off]

            def copy_w1(k, par, e):
                if not early(k, 2):
                    dve.wait_ge(hid_ps, 2 * (k - 1))
                dve.tensor_copy(w1_now[:, par], w1_sb[:, e]).then_inc(w1_copied, 1)

            def upper_act(k, par):
                dve.wait_ge(gelu_done, 2 * k + 2)
                if not early(k, 1):
                    dve.wait_ge(y_ps, k)
                dve.tensor_copy(act_up[:, :, :], actT[:, par]).then_inc(act_upper, 1)

            def lower_w2(k, half, e):
                part = slice(half * FC // 2, (half + 1) * FC // 2)
                dve.wait_ge(w2_upper, 2 * k + half + 1)
                dve.tensor_tensor(w2_low[:, part, :], w2_sb[:, bass.ds(e, 1), part, :],
                                  w2_up[:, part, :].bitcast(F32), ALU.subtract).then_inc(w2_split, 1)

            def finish_block(k, slot, e):
                par = slot % 2
                y = blk_out[:, par, :]
                dve.wait_ge(y_ps, k + 1)
                if not early(k, 2):
                    dve.wait_ge(st_out[par], 8 * (k - par))
                dve.tensor_tensor(y, bank[4 + par][:, 0:E], b2_bc[:, e, :], ALU.add).then_inc(y_biased, 1)
                dve.wait_ge(y_biased, k + 1)
                dve.wait_ge(ld_blk[slot], 16 // RING * (k - slot) + 16)
                dve.scalar_tensor_tensor(out=y, in0=y, scalar=slot_weight[:, bass.ds(k, 1)],
                                         in1=blk_in[:, slot, RES:RES + E], op0=ALU.mult, op1=ALU.add)\
                   .then_inc(blk_done, 1)

            def turn(base, off, slot, known):
                k = base + off
                upper_act(k, slot % 2)
                copy_w1(k + 2, slot % 2, expert_of((base, off + 2), known))
                for half in range(2):
                    lower_w2(k, half, expert_of((base, off), known))
                copy_block(k + 2, slot % 2)
                finish_block(k - 1, (slot - 1) % RING, expert_of((base, off - 1), known))

            for e in range(X):
                dve.wait_ge(ld_w[e], 32)
            first = {}
            copy_w1(0, 0, expert_of((0, 0), first))
            copy_block(0, 0)
            copy_block(1, 1)
            copy_w1(1, 1, expert_of((0, 1), first))
            for half in range(2):
                lower_w2(0, half, expert_of((0, 0), first))
            dve.wait_ge(weights_ps, 1)
            then(dve.tensor_reduce(slot_weight[:, :],
                                   bank[7][:, 0:PIECES * NBLK].rearrange("p (n k) -> p k n", n=PIECES),
                                   AX.X, ALU.add))
            dve.wait_ge(ld_b2, 16)
            upper_act(0, 0)
            dve.wait_ge(act_upper, 1)
            dve.tensor_tensor(act_low[:, :, :], actT[:, 0], act_up[:, :, :].bitcast(F32), ALU.subtract)\
               .then_inc(act_split, 1)
            copy_w1(2, 0, expert_of((0, 2), first))
            copy_block(2, 0)
            for k in range(1, RING):
                turn(0, k, k, first)
            with dve.Fori(1, (NBLK - 2) // RING) as i:
                known = {}
                for n in range(RING):
                    turn(RING * i, n, n, known)
            last = {}
            k = NBLK - 2
            upper_act(k, 0)
            for half in range(2):
                lower_w2(k, half, expert_of((0, k), last))
            dve.wait_ge(hid_ps, 2 * (k + 1))
            dve.tensor_copy(w2_last, w2_sb[:, expert_of((0, k + 1), last)]).then_inc(w2_copied, 1)
            for n in (k - 1, k):
                finish_block(n, n % RING, expert_of((0, n), last))
            finish_block(NBLK - 1, (NBLK - 1) % RING, expert_of((0, NBLK - 1), last))


_INS = ["x", "txt", "L0_tok_ln1_g", "L0_tok_ln1_b", "L0_tok_W_proj", "L0_tok_b_proj", "L0_tok_ln2_g",
        "L0_tok_ln2_b", "L0_tok_cls_token", "L0_tok_pos_emb", "L0_attn_w_attn", "L0_attn_w_proj",
        "L0_ffn_gate_w", "L0_ffn_w1", "L0_ffn_b1", "L0_ffn_w2", "L0_ffn_b2"]


def kernel(**inputs):
    import numpy as _np
    import concourse.bacc as _bacc
    from concourse import mybir as _mybir
    from concourse.bass_utils import run_bass_kernel_spmd as _run

    nc = _bacc.Bacc("TRN2", target_bir_lowering=False, num_devices=1)
    arrays, args = {}, []
    for name in _INS:
        a = _np.ascontiguousarray(inputs[name])
        arrays[f"in_{name}_dram"] = a
        args.append(nc.dram_tensor(f"in_{name}_dram", a.shape, _mybir.dt.from_np(a.dtype),
                                   kind="ExternalInput").ap())
    images, _, _, _ = inputs["x"].shape
    tokens = inputs["L0_tok_pos_emb"].shape[1] + inputs["txt"].shape[1]
    shape = (images, tokens, inputs["txt"].shape[2])
    args.append(nc.dram_tensor("out_0_dram", shape, _mybir.dt.float32, kind="ExternalOutput").ap())
    fusion_program(nc, *args)
    r = _run(nc, [arrays], core_ids=[0])
    return r.results[0]["out_0_dram"]
```
